# Optimizing a Trainium2 kernel written in Bass

```python
import numpy as np
import jax
import jax.numpy as jnp

def _softmax(x, axis=-1):
    return jax.nn.softmax(x, axis=axis)

def _gelu(x):
    return jax.nn.gelu(x, approximate=True)

def _silu(x):
    return jax.nn.silu(x)

def _sigmoid(x):
    return jax.nn.sigmoid(x)

def _layernorm(x, axis=-1, eps=1e-05):
    m = jnp.mean(x, axis=axis, keepdims=True)
    v = jnp.var(x, axis=axis, keepdims=True)
    return (x - m) / jnp.sqrt(v + eps)

def _scatter_add(tgt, idx, src, axis=0):
    return tgt.at[idx].add(src)

def _segment_sum(src, seg, n):
    return jax.ops.segment_sum(src, seg, n)
kernel_name = 'mk_adj_preln_d2_adj_r2_81eb5b'

def setup_inputs(seed: int=0):
    np.random.seed(seed)
    _w = jnp.asarray

    def _rec_inputs():
        import jax
        import jax.numpy as jnp
        _gk = jax.random.key(seed)
        x = -0.0005207 + 1.001 * jax.random.normal(jax.random.fold_in(_gk, 1), (8192, 128), jnp.float32)
        _w = (1.0 + jnp.arange(8192, dtype=jnp.float32)) ** (-0.5)
        _w = _w / _w.mean()
        _pij = jnp.clip(0.000488281 * _w[:, None] * _w[None, :], 0.0, 1.0)
        _a = jax.random.uniform(jax.random.fold_in(_gk, 2), (8192, 8192)) < _pij
        adj = _a.astype(jnp.int32)
        return (x, adj)
    x, adj = _rec_inputs()

    def _L0_gnn_setup():
        import jax, jax.numpy as jnp
        import numpy as np
        N = 4096
        D_IN = 128
        D_OUT = 128
        NEG_INF = -9000000000000000.0
        key = jax.random.key(seed)
        k1, k2, k3, k4 = jax.random.split(key, 4)
        node_features = jax.random.normal(k1, (N, D_IN), dtype=jnp.float32)
        adjacency_matrix = jax.random.randint(k2, (N, N), 0, 2, dtype=jnp.int32)
        W = jax.random.normal(k3, (D_OUT, D_IN), dtype=jnp.float32) / np.sqrt(D_IN)
        b_W = jnp.zeros((D_OUT,), dtype=jnp.float32)
        a_vec = jax.random.normal(k4, (2 * D_OUT,), dtype=jnp.float32) / np.sqrt(2 * D_OUT)
        b_a = jnp.zeros((1,), dtype=jnp.float32)
        return {'node_features': node_features, 'adjacency_matrix': adjacency_matrix, 'W': W, 'b_W': b_W, 'a_vec': a_vec, 'b_a': b_a}
    _L0_gnn_all = _L0_gnn_setup()
    _L0_gnn_in = {k: v for k, v in _L0_gnn_all.items() if k in ('W', 'b_W', 'a_vec', 'b_a')}
    del _L0_gnn_all

    def _L1_gnn_setup():
        import jax, jax.numpy as jnp
        import numpy as np
        N, F_IN, F_OUT = (4096, 128, 128)
        ALPHA = 0.2
        NEG = -9000000000000000.0
        key = jax.random.key(seed)
        k1, k2, k3, k4, k5 = jax.random.split(key, 5)
        h = jax.random.normal(k1, (N, F_IN), dtype=jnp.float32)
        adj = jax.random.randint(k2, (N, N), 0, 2, dtype=jnp.int32)
        W_w = jax.random.normal(k3, (F_IN, F_OUT), dtype=jnp.float32) / np.sqrt(F_IN)
        W_b = jax.random.normal(k4, (F_OUT,), dtype=jnp.float32) * 0.01
        a = jax.random.normal(k5, (2 * F_OUT, 1), dtype=jnp.float32) / np.sqrt(2 * F_OUT)
        return {'h': h, 'adj': adj, 'W_w': W_w, 'W_b': W_b, 'a': a}
    _L1_gnn_all = _L1_gnn_setup()
    _L1_gnn_in = {k: v for k, v in _L1_gnn_all.items() if k in ('W_w', 'W_b', 'a')}
    del _L1_gnn_all
    return {'x': x, 'adj': adj, 'L0_gnn_W': _L0_gnn_in['W'], 'L0_gnn_b_W': _L0_gnn_in['b_W'], 'L0_gnn_a_vec': _L0_gnn_in['a_vec'], 'L0_gnn_b_a': _L0_gnn_in['b_a'], 'L1_gnn_W_w': _L1_gnn_in['W_w'], 'L1_gnn_W_b': _L1_gnn_in['W_b'], 'L1_gnn_a': _L1_gnn_in['a']}

def reference(x, adj, L0_gnn_W, L0_gnn_b_W, L0_gnn_a_vec, L0_gnn_b_a, L1_gnn_W_w, L1_gnn_W_b, L1_gnn_a):
    import jax
    import jax.numpy as jnp

    def _L0_gnn_ref(node_features, adjacency_matrix, W, b_W, a_vec, b_a):
        import jax, jax.numpy as jnp
        import numpy as np
        N = 4096
        D_IN = 128
        D_OUT = 128
        NEG_INF = -9000000000000000.0
        h = node_features @ W.T + b_W
        a1, a2 = (a_vec[:D_OUT], a_vec[D_OUT:])
        e = (h @ a1)[:, None] + (h @ a2)[None, :] + b_a[0]
        e = jnp.where(e > 0, e, 0.2 * e)
        scores = jnp.where(adjacency_matrix > 0, e, jnp.float32(NEG_INF))
        attention = jax.nn.softmax(scores, axis=1)
        h_prime = attention @ h
        return h_prime

    def _L1_gnn_ref(h, adj, W_w, W_b, a):
        import jax, jax.numpy as jnp
        import numpy as np
        N, F_IN, F_OUT = (4096, 128, 128)
        ALPHA = 0.2
        NEG = -9000000000000000.0
        Wh = h @ W_w + W_b
        a1 = a[:F_OUT, 0]
        a2 = a[F_OUT:, 0]
        e = jax.nn.leaky_relu((Wh @ a1)[:, None] + (Wh @ a2)[None, :], negative_slope=ALPHA)
        attention = jnp.where(adj > 0, e, NEG)
        attention = jax.nn.softmax(attention, axis=1)
        h_prime = attention @ Wh
        return h_prime
    h = jnp.maximum(_layernorm(x, axis=-1), 0.0)
    x = x + _L0_gnn_ref(h, adj, L0_gnn_W, L0_gnn_b_W, L0_gnn_a_vec, L0_gnn_b_a)
    h = jnp.maximum(_layernorm(x, axis=-1), 0.0)
    x = x + _L1_gnn_ref(h, adj, L1_gnn_W_w, L1_gnn_W_b, L1_gnn_a)
    return x

_drawn_inputs = setup_inputs


def setup_inputs(seed=0):
    import zlib

    import numpy as np

    out = dict(_drawn_inputs(seed))
    spreads = {'L0_gnn_b_W': (0.0, 0.1)}
    factors = {'L1_gnn_W_b': 6.954}
    for name, (base, spread) in spreads.items():
        noise = np.random.default_rng([zlib.crc32(name.encode()), seed]).standard_normal(out[name].shape)
        drawn = base * np.exp(spread * noise) if base else spread * noise
        out[name] = jnp.asarray(drawn.astype(out[name].dtype))
    for name, factor in factors.items():
        out[name] = (out[name] * factor).astype(out[name].dtype)
    return out
```

```python
import concourse.bass as bass
from concourse import mybir
from contextlib import ExitStack
import math

NODES = 8192
DIM = 128
LAYERS = 2
EPS = 1e-5
TILE = 128
TILES = NODES // TILE
QUADS = 4
QROWS = 32
SPAN = NODES // QUADS
RGROUPS = TILE // QROWS
BYTES = 4
BLOCKS = SPAN // (QROWS * BYTES)
CHUNKS = BLOCKS * BYTES
ONE = DIM
NEG_S, POS_T, LOG_B, LOG_D = DIM + 1, DIM + 2, DIM + 3, DIM + 4
EXT = DIM + 5
PART = DIM + 1
ROW = 2 * PART
KAPPA = 4.0
LEAK = 0.2
G1_WORD = 0x20202020
G2_WORD = 0x10101010
VGROUPS = 4
HEAD = 4
TAIL = 62


class Tile:

    def __init__(self, k, u=None):
        self.k, self.u, self.p = k, u, k % 2
        self.t = k if u is None else 2 * u + k
        self.n = k // 2 if u is None else u + k // 2

    def plus(self, d):
        return Tile(self.k + d, self.u)

    @property
    def exists(self):
        return self.u is not None or 0 <= self.k < TILES

    def wait_before(self, eng, sem, back):
        if self.u is not None or self.k - back >= 0:
            eng.wait_ge(sem, self.t - back + 1)


def sweep(eng, body, trail=0):
    for k in range(HEAD):
        body(Tile(k))
    with eng.Fori(HEAD // 2, TAIL // 2) as u:
        for k in range(2):
            body(Tile(k, u))
    for k in range(TAIL, TILES + trail):
        body(Tile(k))


def gat_kernel(nc, x, adj, w_0, b_w_0, a_vec_0, b_a_0, w_1, b_w_1, a_1, out):
    F32, F16, I8, I32, U32, FP8 = (mybir.dt.float32, mybir.dt.float16, mybir.dt.int8, mybir.dt.int32,
                                   mybir.dt.uint32, mybir.dt.float8e4)
    ALU, ACT, AX = mybir.AluOpType, mybir.ActivationFunctionType, mybir.AxisListType
    ds = bass.ds

    mask_dram = nc.dram_tensor("mask_bytes", (TILES, 128, NODES), I8, kind="Internal").ap()
    rows_dram = [nc.dram_tensor(f"node_rows_{l}", (TILES, TILE, 2 * ROW), F16, kind="Internal").ap() for l in range(LAYERS)]
    st_dram = [nc.dram_tensor(f"neg_s_and_t_{l}", (2, NODES), F32, kind="Internal").ap() for l in range(LAYERS)]
    x1_dram = nc.dram_tensor("x_after_layer_0", (NODES, DIM), F32, kind="Internal").ap()

    with ExitStack() as ctx:
        def sb(name, shape, dt):
            return ctx.enter_context(nc.sbuf_tensor(name, shape, dt))

        def ps(name):
            return ctx.enter_context(nc.psum_tensor(name, [128, 512], F32))

        def sem(name):
            return ctx.enter_context(nc.semaphore(name))

        adj_sb = sb("adj_sb", [128, RGROUPS, SPAN], I32)
        sign_a = sb("sign_a", [128, 2, NODES], I8)
        sign_z = sb("sign_z", [128, 2, NODES], I8)
        g1 = sb("g1", [128, 2, NODES], I8)
        g2 = sb("g2", [128, 2, NODES], I8)
        t_row = sb("t_row", [128, SPAN], F32)
        node_rows = sb("node_rows", [128, CHUNKS, 2 * ROW], F16)
        x_all = node_rows[:].rearrange("p c r -> p (c r)")[:, 0:2 * TILES * DIM].bitcast(F32) \
                            .rearrange("p (t d) -> p t d", d=DIM)
        nat = sb("nat", [128, 2 * TILES], F32)
        nat_t = sb("nat_t", [128, TILE], F32)
        s_strip = sb("s_strip", [128, TILES * RGROUPS], F32)
        neg_s = sb("neg_s", [128, TILES * RGROUPS], F32)
        coef_a = sb("coef_a", [128, TILES], F32)
        coef_c = sb("coef_c", [128, TILES], F32)
        h_mean = sb("h_mean", [128, DIM], F32)
        h_max = sb("h_max", [128, LAYERS, TILES], F32)
        part_a = sb("part_a", [128, 2, ROW], F32)
        part_ac = sb("part_ac", [128, 2, ROW], F32)
        joined = sb("joined", [128, 2, PART], F32)
        empty = sb("empty", [128, 2, 1], F32)
        den = sb("den", [128, 2, 1], F32)
        rden = sb("rden", [128, 2, 1], F32)
        numer = sb("numer", [128, 2, DIM], F32)
        x_old = sb("x_old", [128, 2, DIM], F32)
        x_new = sb("x_new", [128, 2, DIM], F32)
        stats = sb("stats", [128, 2, 6], F32)
        mean_var = sb("mean_var", [128, 2, 2], F32)
        var_eps = sb("var_eps", [128, 2, 1], F32)
        rstd = sb("rstd", [128, 2, 1], F32)
        centred = sb("centred", [128, 2, DIM], F32)
        centred_t = sb("centred_t", [128, 2, DIM], F32)
        ext = sb("ext", [128, 2, EXT], F32)
        b_and_d = sb("b_and_d", [128, 2, 2], F32)
        row_parts = sb("row_parts", [128, 2, 2 * ROW], F16)
        ident = sb("ident", [128, 128], F32)
        averager = sb("averager", [128, 128], F32)
        minus_half = sb("minus_half", [128, 1], F32)
        w_raw = [sb(f"w_raw_{l}", [128, 128], F32) for l in range(LAYERS)]
        w_tr = [sb(f"w_tr_{l}", [128, 128], F32) for l in range(LAYERS)]
        a_raw = [sb(f"a_raw_{l}", [128, 2], F32) for l in range(LAYERS)]
        b_raw = [sb(f"b_raw_{l}", [128, 1], F32) for l in range(LAYERS)]
        b_a_sb = sb("b_a_sb", [128, 1], F32)
        b_wide = [sb(f"b_wide_{l}", [128, 128], F32) for l in range(LAYERS)]
        id_and_a = [sb(f"id_and_a_{l}", [128, EXT], F32) for l in range(LAYERS)]
        w_ext = [sb(f"w_ext_{l}", [128, EXT], F32) for l in range(LAYERS)]
        bias = [sb(f"bias_{l}", [128, EXT], F32) for l in range(LAYERS)]

        acc = [[ps(f"acc_{p}_{s}") for s in range(2)] for p in range(2)]
        ps_t = [ps(f"ps_t_{p}") for p in range(2)]
        ps_h = ps("ps_h")
        ps_mean = ps("ps_mean")

        weights_loaded, ident_ready = sem("weights_loaded"), sem("ident_ready")
        setup_pe, setup_dve = sem("setup_pe"), sem("setup_dve")
        x_loaded = sem("x_loaded")
        adj_loaded = [sem(f"adj_loaded_{r}") for r in range(RGROUPS)]
        cast_done = sem("cast_done")
        mask_stored = [sem(f"mask_stored_{p}") for p in range(2)]
        mask_loaded = [sem(f"mask_loaded_{p}") for p in range(2)]

        class LayerSems:
            def __init__(self, l):
                self.zsign_act, self.zsign_dve = sem(f"zsign_act_{l}"), sem(f"zsign_dve_{l}")
                self.edge_bits, self.turned = sem(f"edge_bits_{l}"), sem(f"turned_{l}")
                self.g1_ready, self.g_ready = sem(f"g1_ready_{l}"), sem(f"g_ready_{l}")
                self.tile_summed = sem(f"tile_summed_{l}")
                self.part_a, self.part_ac, self.fin = sem(f"part_a_{l}"), sem(f"part_ac_{l}"), sem(f"fin_{l}")
                self.x_old = [sem(f"x_old_{l}_{p}") for p in range(2)]
                self.x_stored = [sem(f"x_stored_{l}_{p}") for p in range(2)]
                self.stats, self.mean_var = sem(f"stats_{l}"), sem(f"mean_var_{l}")
                self.centred, self.var_eps, self.rstd = sem(f"centred_{l}"), sem(f"var_eps_{l}"), sem(f"rstd_{l}")
                self.turned_ps, self.centred_t = sem(f"turned_ps_{l}"), sem(f"centred_t_{l}")
                self.h_raw, self.ext, self.h_max = sem(f"h_raw_{l}"), sem(f"ext_{l}"), sem(f"h_max_{l}")
                self.mean_sum, self.st_kept = sem(f"mean_sum_{l}"), sem(f"st_kept_{l}")
                self.b_and_d, self.high, self.low = sem(f"b_and_d_{l}"), sem(f"high_{l}"), sem(f"low_{l}")
                self.rows_stored = [sem(f"rows_stored_{l}_{p}") for p in range(2)]
                self.nat_ps, self.nat_sb, self.nat_stored = sem(f"nat_ps_{l}"), sem(f"nat_sb_{l}"), sem(f"nat_stored_{l}")
                self.t_row, self.s_strip = sem(f"t_row_{l}"), sem(f"s_strip_{l}")
                self.neg_s, self.mean_kept, self.coefs = sem(f"neg_s_{l}"), sem(f"mean_kept_{l}"), sem(f"coefs_{l}")
                self.rows_loaded = [sem(f"rows_loaded_{l}_{g}") for g in range(VGROUPS)]

        S = [LayerSems(l) for l in range(LAYERS)]
        x_src = [x, x1_dram]
        x_dst = [x1_dram, out]
        FIN = 6

        def x_of(l, T):
            return x_all[:, ds(T.t, 1), :].rearrange("p o d -> p (o d)") if l == 0 else x_new[:, T.p, :]

        block = ctx.enter_context(nc.Block())

        @block.sync
        def _(sp):
            def load_adj(T, r):
                for a in range(QUADS):
                    sp.nop(nofuse=True)
                    sp.dma_start(adj_sb[QROWS * a:QROWS * (a + 1), r, :],
                                 adj[ds(T.t * TILE + QROWS * r, QROWS), SPAN * a:SPAN * (a + 1)]) \
                      .then_inc(adj_loaded[r], 16)

            def load_x_old(l, T):
                if T.u is not None or T.k >= 2:
                    sp.wait_ge(S[l].fin, FIN * (T.t - 1))
                sp.nop(nofuse=True)
                sp.dma_start(x_old[:, T.p, :], x_src[l][ds(T.t * TILE, TILE), :]).then_inc(S[l].x_old[T.p], 16)

            def store_x_new(l, T):
                sp.wait_ge(S[l].fin, FIN * (T.t + 1))
                sp.nop(nofuse=True)
                sp.dma_start(x_dst[l][ds(T.t * TILE, TILE), :], x_new[:, T.p, :]).then_inc(S[l].x_stored[T.p], 16)

            def store_rows(l, T):
                sp.wait_ge(S[l].low, T.t + 1)
                sp.nop(nofuse=True)
                sp.dma_start(rows_dram[l][ds(T.t, 1), :, :].rearrange("o p r -> p (o r)"), row_parts[:, T.p, :]) \
                  .then_inc(S[l].rows_stored[T.p], 16)

            def spread_layer(l):
                sp.wait_ge(S[l].nat_sb, 1)
                sp.dma_start(st_dram[l].rearrange("c (t m) -> (c t) m", m=TILE), nat_t[:]).then_inc(S[l].nat_stored, 16)
                sp.wait_ge(S[l].nat_stored, 16)
                if l:
                    sp.wait_ge(S[l - 1].zsign_dve, 2 * TILES)
                    sp.wait_ge(S[l - 1].zsign_act, 2 * TILES)
                for a in range(QUADS):
                    quad = slice(QROWS * a, QROWS * (a + 1))
                    sp.dma_start(s_strip[quad, :].rearrange("p (g i) -> p g i", i=QROWS),
                                 st_dram[l][0, :].rearrange("(g p i) -> p g i", p=QROWS, i=QROWS)).then_inc(S[l].s_strip, 16)
                    sp.dma_start(t_row[quad, :],
                                 st_dram[l][1, SPAN * a:SPAN * (a + 1)].partition_broadcast(QROWS)).then_inc(S[l].t_row, 16)
                for p in range(2):
                    sp.wait_ge(S[l].rows_stored[p], 16 * TILES // 2)
                if l == 0:
                    sp.wait_ge(S[0].centred, TILES)
                    sp.wait_ge(S[0].stats, TILES)
                else:
                    sp.wait_ge(S[l - 1].tile_summed, TILES)
                per = BLOCKS // VGROUPS
                for g in range(VGROUPS):
                    for a in range(QUADS):
                        src = rows_dram[l][BLOCKS * a + per * g:BLOCKS * a + per * (g + 1), :, :]
                        dst = node_rows[QROWS * a:QROWS * (a + 1), BYTES * per * g:BYTES * per * (g + 1), :]
                        sp.dma_start(dst.rearrange("p (b k) r -> p b (k r)", k=BYTES),
                                     src.rearrange("b (j k) r -> j b (k r)", k=BYTES)).then_inc(S[l].rows_loaded[g], 16)

            sp.dma_start(w_raw[0][:], w_0).then_inc(weights_loaded, 16)
            sp.dma_start(w_raw[1][:], w_1).then_inc(weights_loaded, 16)
            with nc.allow_non_contiguous_dma(reason="weight vectors onto partitions, once"):
                sp.dma_start(a_raw[0][:], a_vec_0.rearrange("(c p) -> p c", p=DIM)).then_inc(weights_loaded, 16)
                sp.dma_start(a_raw[1][:], a_1.rearrange("(c p) o -> p (c o)", p=DIM)).then_inc(weights_loaded, 16)
                sp.dma_start(b_raw[0][:], b_w_0.rearrange("(p o) -> p o", o=1)).then_inc(weights_loaded, 16)
                sp.dma_start(b_raw[1][:], b_w_1.rearrange("(p o) -> p o", o=1)).then_inc(weights_loaded, 16)
                sp.dma_start(b_a_sb[:], b_a_0.partition_broadcast(128)).then_inc(weights_loaded, 16)
            x_tiles = x.rearrange("(t m) d -> m t d", m=TILE)
            for g in range(8):
                sp.dma_start(x_all[:, 8 * g:8 * g + 8, :], x_tiles[:, 8 * g:8 * g + 8, :]).then_inc(x_loaded, 16)
                sp.wait_ge(x_loaded, 16 * (g + 1))
            for r in range(RGROUPS):
                load_adj(Tile(0), r)
            sweep(sp, lambda T: store_rows(0, T))
            spread_layer(0)

            load_x_old(0, Tile(0))
            load_x_old(0, Tile(1))

            def layer_0_tile(T):
                if T.plus(1).exists:
                    for r in range(RGROUPS):
                        sp.wait_ge(cast_done, RGROUPS * T.t + r + 1)
                        load_adj(T.plus(1), r)
                sp.wait_ge(cast_done, RGROUPS * (T.t + 1))
                sp.nop(nofuse=True)
                sp.dma_start(mask_dram[ds(T.t, 1), :, :].rearrange("o p c -> p (o c)"), sign_a[:, T.p, :]) \
                  .then_inc(mask_stored[T.p], 16)
                if T.plus(-3).exists:
                    store_x_new(0, T.plus(-3))
                    load_x_old(0, T.plus(-1))
                    store_rows(1, T.plus(-3))

            sweep(sp, layer_0_tile)
            load_x_old(0, Tile(TILES - 1))
            for k in range(TILES - 3, TILES):
                store_x_new(0, Tile(k))
                store_rows(1, Tile(k))

            def load_mask(T):
                T.wait_before(sp, S[1].edge_bits, 2)
                sp.nop(nofuse=True)
                sp.dma_start(sign_a[:, T.p, :], mask_dram[ds(T.t, 1), :, :].rearrange("o p c -> p (o c)")) \
                  .then_inc(mask_loaded[T.p], 16)

            sp.wait_ge(S[0].edge_bits, TILES)
            for p in range(2):
                sp.wait_ge(mask_stored[p], 16 * TILES // 2)
            load_mask(Tile(0))
            load_mask(Tile(1))
            for p in range(2):
                sp.wait_ge(S[0].x_stored[p], 16 * TILES // 2)
            spread_layer(1)
            load_x_old(1, Tile(0))
            load_x_old(1, Tile(1))

            def layer_1_tile(T):
                if T.plus(2).exists:
                    load_mask(T.plus(2))
                if T.plus(-2).exists:
                    store_x_new(1, T.plus(-2))
                    load_x_old(1, T)

            for k in range(HEAD):
                layer_1_tile(Tile(k))
            with sp.Fori(HEAD // 2, TAIL // 2) as u:
                for k in range(2):
                    layer_1_tile(Tile(k, u))
            for k in range(TAIL, TILES):
                layer_1_tile(Tile(k))
            store_x_new(1, Tile(TILES - 2))
            store_x_new(1, Tile(TILES - 1))
            for p in range(2):
                sp.wait_ge(S[1].x_stored[p], 16 * TILES // 2)

        @block.gpsimd
        def _(pool):
            pool.memset(minus_half[:], -0.5).then_inc(ident_ready, 1)
            pool.memset(averager[:], 1.0 / NODES).then_inc(ident_ready, 1)
            pool.memset(ident[:], 0.0).then_inc(ident_ready, 1)
            pool.wait_ge(ident_ready, 3)
            pool.affine_select(out=ident[:], in_=ident[:], compare_op=ALU.not_equal, fill=1.0, base=0,
                               pattern=[[-1, 128]], channel_multiplier=1).then_inc(ident_ready, 1)

            nat_v = nat[:].rearrange("p (c t) -> p c t", c=2)

            def node_step(l, T):
                pool.wait_ge(S[l].var_eps, T.t + 1)
                T.wait_before(pool, S[l].ext, 2)
                pool.nop(nofuse=True)
                pool.tensor_tensor(rstd[:, T.p, :], var_eps[:, T.p, :], minus_half[:], ALU.pow).then_inc(S[l].rstd, 1)

            def keep_st(l, T):
                pool.wait_ge(S[l].ext, T.t + 1)
                pool.tensor_copy(nat_v[:, :, ds(T.t, 1)], ext[:, T.p, NEG_S:POS_T + 1].rearrange("p (c o) -> p c o", o=1)) \
                    .then_inc(S[l].st_kept, 1)

            for l in range(LAYERS):
                if l:
                    pool.wait_ge(S[0].nat_ps, 1)
                    pool.wait_ge(S[0].coefs, 2)

                def body(T):
                    if T.exists:
                        node_step(l, T)
                    if T.plus(-1).exists:
                        keep_st(l, T.plus(-1))

                sweep(pool, body, trail=1)

        @block.tensor
        def _(pe):
            pe.wait_ge(weights_loaded, 7 * 16)
            pe.wait_ge(ident_ready, 4)
            for l in range(LAYERS):
                pe.transpose(ps_t[l][:, 0:128], w_raw[l][:], ident[:]).then_inc(setup_pe, 1)
            pe.wait_ge(setup_dve, LAYERS)
            w_oi = [w_raw[0], w_tr[1]]
            for l in range(LAYERS):
                pe.matmul(ps_h[:, 8 * l:8 * l + 5], w_oi[l][:], id_and_a[l][:, DIM:EXT], start=True, stop=True) \
                  .then_inc(setup_pe, 1)
                pe.matmul(acc[0][l][:, 0:EXT], b_wide[l][:], id_and_a[l][:], start=True, stop=True).then_inc(setup_pe, 1)
            pe.wait_ge(setup_dve, 2 * LAYERS)

            def turn(l, T):
                pe.wait_ge(S[l].centred, T.t + 1)
                T.wait_before(pe, S[l].centred_t, 2)
                pe.transpose(ps_t[T.p][:, 0:DIM], centred[:, T.p, :], ident[:]).then_inc(S[l].turned_ps, 1)

            def project(l, T):
                pe.wait_ge(S[l].centred_t, T.t + 1)
                T.wait_before(pe, S[l].ext, 1)
                pe.matmul(ps_h[:, 0:EXT], centred_t[:, T.p, :], w_ext[l][:], start=True, stop=True).then_inc(S[l].h_raw, 1)

            def add_mean(l, T):
                pe.wait_ge(S[l].ext, T.t + 1)
                first, last = (T.u is None and T.k == 0), (T.u is None and T.k == TILES - 1)
                pe.matmul(ps_mean[:, 0:DIM], averager[:], ext[:, T.p, 0:DIM], start=first, stop=last,
                          skip_group_check=True).then_inc(S[l].mean_sum, 1)

            def close_nodes(l):
                pe.wait_ge(S[l].st_kept, TILES)
                pe.wait_ge(S[l].centred_t, TILES)
                pe.transpose(ps_t[0][:, 0:128], nat[:], ident[:]).then_inc(S[l].nat_ps, 1)

            def first_nodes(T):
                if T.u is None and T.k == 0:
                    turn(0, T)
                if T.plus(1).exists:
                    turn(0, T.plus(1))
                project(0, T)
                if T.plus(-1).exists:
                    add_mean(0, T.plus(-1))

            sweep(pe, first_nodes)
            add_mean(0, Tile(TILES - 1))
            close_nodes(0)

            turn_at, project_at, mean_at = 26, 38, 52

            for l in range(LAYERS):
                def tile(T):
                    pe.wait_ge(S[l].g_ready, T.t + 1)
                    T.wait_before(pe, S[l].part_a, 2)
                    T.wait_before(pe, S[l].part_ac, 2)
                    pe.nop(nofuse=True)
                    stationary = [m[:, T.p, :].bitcast(FP8).rearrange("p (b i k) -> p b k i", b=BLOCKS, k=BYTES)
                                  for m in (g1, g2)]
                    for c in range(CHUNKS):
                        if T.u is None and T.k == 0 and c % (CHUNKS // VGROUPS) == 0:
                            pe.wait_ge(S[l].rows_loaded[c // (CHUNKS // VGROUPS)], 16 * QUADS)
                        for s in range(2):
                            mm = pe.matmul(acc[T.p][s][:, 0:ROW], stationary[s][:, c // BYTES, c % BYTES, :],
                                           node_rows[:, c, ROW * s:ROW * (s + 1)],
                                           start=(c == 0), stop=(c == CHUNKS - 1), skip_group_check=True)
                        if l == 0 and T.plus(-1).exists:
                            if c == turn_at:
                                turn(1, T.plus(-1))
                            if c == project_at:
                                project(1, T.plus(-1))
                            if c == mean_at:
                                add_mean(1, T.plus(-1))
                    mm.then_inc(S[l].tile_summed, 1)

                if l == 0:
                    pe.wait_ge(S[0].mean_kept, 1)
                    pe.wait_ge(S[0].nat_sb, 1)
                sweep(pe, tile)
                if l == 0:
                    last = Tile(TILES - 1)
                    turn(1, last)
                    project(1, last)
                    add_mean(1, last)
                    close_nodes(1)

        @block.scalar
        def _(act):
            def node_copy(l, T):
                act.wait_ge(S[l].turned_ps, T.t + 1)
                T.wait_before(act, S[l].h_raw, 2)
                nc.scalar.copy(centred_t[:, T.p, :], ps_t[T.p][:, 0:DIM]).then_inc(S[l].centred_t, 1)

            def node_high(l, T):
                act.wait_ge(S[l].ext, T.t + 1)
                T.wait_before(act, S[l].high, 2)
                T.wait_before(act, S[l].low, 2)
                if T.u is not None or T.k >= 2:
                    act.wait_ge(S[l].rows_stored[T.p], 16 * T.n)
                nc.scalar.activation(b_and_d[:, T.p, :], ext[:, T.p, LOG_B:LOG_D + 1], ACT.Exp).then_inc(S[l].b_and_d, 1)
                act.wait_ge(S[l].b_and_d, T.t + 1)
                for s in range(2):
                    last = nc.scalar.activation(row_parts[:, T.p, ROW * s:ROW * s + PART], ext[:, T.p, 0:PART], ACT.Copy,
                                                scale=b_and_d[:, T.p, s:s + 1])
                last.then_inc(S[l].high, 1)

            def cast(T):
                if T.u is not None or T.k >= 2:
                    act.wait_ge(S[0].edge_bits, T.t - 1)
                    act.wait_ge(mask_stored[T.p], 16 * T.n)
                for r in range(RGROUPS):
                    act.wait_ge(adj_loaded[r], 16 * QUADS * (T.t + 1))
                    nc.scalar.activation(sign_a[:, T.p, SPAN * r:SPAN * (r + 1)], adj_sb[:, r, :], ACT.Sign, scale=-1.0) \
                      .then_inc(cast_done, 1)

            def z_sign(l, T):
                T.wait_before(act, S[l].turned, 2)
                for r in range(2):
                    nc.scalar.activation(sign_z[:, T.p, SPAN * r:SPAN * (r + 1)], t_row[:], ACT.Sign, scale=-1.0,
                                         bias=neg_s[:, ds(RGROUPS * T.t + r, 1)]).then_inc(S[l].zsign_act, 1)

            def part_one(l, T):
                act.wait_ge(S[l].tile_summed, T.t + 1)
                T.wait_before(act, S[l].part_ac, 2)
                nc.scalar.activation(part_a[:, T.p, :], acc[T.p][0][:, 0:ROW], ACT.Copy, scale=coef_a[:, ds(T.t, 1)]) \
                  .then_inc(S[l].part_a, 1)

            def open_layer(l):
                act.wait_ge(S[l].st_kept, TILES)
                if l:
                    act.wait_ge(S[l - 1].part_ac, TILES)
                    act.wait_ge(S[l - 1].part_a, TILES)
                nc.scalar.activation(coef_a[:], nat[:, 0:TILES], ACT.Exp, scale=-1.0).then_inc(S[l].coefs, 1)
                nc.scalar.activation(coef_c[:], nat[:, 0:TILES], ACT.Exp, scale=-LEAK).then_inc(S[l].coefs, 1)

            def first_nodes(T):
                if T.u is None and T.k == 0:
                    node_copy(0, T)
                if T.plus(1).exists:
                    node_copy(0, T.plus(1))
                node_high(0, T)

            sweep(act, first_nodes)
            cast(Tile(0))
            cast(Tile(1))
            open_layer(0)
            act.wait_ge(S[0].neg_s, 1)
            act.wait_ge(S[0].t_row, 16 * QUADS)
            act.wait_ge(S[0].coefs, 2)
            z_sign(0, Tile(0))
            z_sign(0, Tile(1))

            def layer_0_tile(T):
                if T.plus(-1).exists:
                    part_one(0, T.plus(-1))
                if T.plus(2).exists:
                    cast(T.plus(2))
                    z_sign(0, T.plus(2))
                if T.plus(-1).exists:
                    node_copy(1, T.plus(-1))
                    node_high(1, T.plus(-1))

            sweep(act, layer_0_tile, trail=1)
            open_layer(1)
            act.wait_ge(S[1].neg_s, 1)
            act.wait_ge(S[1].t_row, 16 * QUADS)
            act.wait_ge(S[1].coefs, 2)
            act.wait_ge(S[0].turned, TILES)
            z_sign(1, Tile(0))
            z_sign(1, Tile(1))

            def layer_1_tile(T):
                if T.plus(-1).exists:
                    part_one(1, T.plus(-1))
                if T.plus(2).exists:
                    z_sign(1, T.plus(2))

            sweep(act, layer_1_tile, trail=1)

        @block.vector
        def _(dve):
            dve.wait_ge(weights_loaded, 7 * 16)
            dve.wait_ge(ident_ready, 4)
            steps = sem("setup_steps")
            n_steps = [0]

            def step(ins):
                n_steps[0] += 1
                ins.then_inc(steps, 1)
                dve.wait_ge(steps, n_steps[0])

            for l in range(LAYERS):
                ia = id_and_a[l]
                step(nc.vector.tensor_copy(ia[:, 0:DIM], ident[:]))
                step(nc.vector.memset(ia[:, ONE:ONE + 1], 0.0))
                step(nc.vector.tensor_scalar(ia[:, NEG_S:NEG_S + 1], a_raw[l][:, 0:1], -1.0, None, ALU.mult))
                step(nc.vector.tensor_copy(ia[:, POS_T:POS_T + 1], a_raw[l][:, 1:2]))
                step(nc.vector.tensor_copy(ia[:, LOG_B:LOG_B + 1], a_raw[l][:, 1:2]))
                step(nc.vector.tensor_scalar(ia[:, LOG_D:LOG_D + 1], a_raw[l][:, 1:2], LEAK, None, ALU.mult))
                step(nc.vector.tensor_scalar(b_wide[l][:], ident[:], 0.0, b_raw[l][:, 0:1], ALU.mult, ALU.add))
                dve.wait_ge(setup_pe, l + 1)
                nc.vector.tensor_copy(w_tr[l][:], ps_t[l][:, 0:128]).then_inc(setup_dve, 1)
            dve.wait_ge(setup_dve, LAYERS)
            w_io = [w_tr[0], w_raw[1]]
            for l in range(LAYERS):
                dve.wait_ge(setup_pe, 3 * LAYERS)
                step(nc.vector.tensor_copy(w_ext[l][:, 0:DIM], w_io[l][:]))
                step(nc.vector.tensor_copy(w_ext[l][:, DIM:EXT], ps_h[:, 8 * l:8 * l + 5]))
                step(nc.vector.tensor_copy(bias[l][:], acc[0][l][:, 0:EXT]))
                step(nc.vector.tensor_scalar(bias[l][:, ONE:ONE + 1], bias[l][:, ONE:ONE + 1], 1.0, None, ALU.add))
                if l == 0:
                    step(nc.vector.tensor_tensor(bias[0][:, NEG_S:NEG_S + 1], bias[0][:, NEG_S:NEG_S + 1], b_a_sb[:],
                                                 ALU.subtract))
                nc.vector.tensor_scalar(bias[l][:, LOG_B:EXT], bias[l][:, LOG_B:EXT], math.log(KAPPA), None, ALU.add) \
                  .then_inc(setup_dve, 1)
            dve.wait_ge(setup_dve, 2 * LAYERS)

            def node_stats(l, T):
                T.wait_before(dve, S[l].mean_var, 2)
                nc.vector.bn_stats(stats[:, T.p, :], x_of(l, T)).then_inc(S[l].stats, 1)
                dve.wait_ge(S[l].stats, T.t + 1)
                T.wait_before(dve, S[l].centred, 2)
                T.wait_before(dve, S[l].var_eps, 2)
                dve.nop(nofuse=True)
                nc.vector.bn_aggr(mean_var[:, T.p, :], stats[:, T.p, :]).then_inc(S[l].mean_var, 1)
                dve.wait_ge(S[l].mean_var, T.t + 1)
                T.wait_before(dve, S[l].turned_ps, 2)
                nc.vector.tensor_scalar(centred[:, T.p, :], x_of(l, T), mean_var[:, T.p, 0:1], 0.0, ALU.subtract, ALU.max) \
                    .then_inc(S[l].centred, 1)
                T.wait_before(dve, S[l].rstd, 2)
                nc.vector.tensor_scalar(var_eps[:, T.p, :], mean_var[:, T.p, 1:2], EPS, None, ALU.add) \
                    .then_inc(S[l].var_eps, 1)

            def node_ext(l, T):
                dve.wait_ge(S[l].h_raw, T.t + 1)
                dve.wait_ge(S[l].rstd, T.t + 1)
                T.wait_before(dve, S[l].high, 2)
                T.wait_before(dve, S[l].mean_sum, 2)
                T.wait_before(dve, S[l].st_kept, 2)
                T.wait_before(dve, S[l].h_max, 2)
                T.wait_before(dve, S[l].low, 2)
                nc.vector.scalar_tensor_tensor(out=ext[:, T.p, :], in0=ps_h[:, 0:EXT], scalar=rstd[:, T.p, 0:1],
                                               in1=bias[l][:], op0=ALU.mult, op1=ALU.add).then_inc(S[l].ext, 1)

            def node_max(l, T):
                dve.wait_ge(S[l].ext, T.t + 1)
                nc.vector.tensor_reduce(out=h_max[:, l, ds(T.t, 1)], in_=ext[:, T.p, 0:DIM], axis=AX.X, op=ALU.max,
                                        apply_absolute_value=True).then_inc(S[l].h_max, 1)

            def node_low(l, T):
                dve.wait_ge(S[l].high, T.t + 1)
                for s in range(2):
                    last = nc.vector.scalar_tensor_tensor(
                        out=row_parts[:, T.p, ROW * s + PART:ROW * (s + 1)], in0=ext[:, T.p, 0:PART],
                        scalar=b_and_d[:, T.p, s:s + 1], in1=row_parts[:, T.p, ROW * s:ROW * s + PART],
                        op0=ALU.mult, op1=ALU.subtract)
                last.then_inc(S[l].low, 1)

            def z_sign(l, T):
                if T.u is None and T.k < 2 and l:
                    dve.wait_ge(S[l - 1].turned, TILES)
                T.wait_before(dve, S[l].turned, 2)
                for r in range(2, RGROUPS):
                    nc.vector.tensor_scalar(sign_z[:, T.p, SPAN * r:SPAN * (r + 1)], t_row[:],
                                            neg_s[:, ds(RGROUPS * T.t + r, 1)], -1.0, ALU.is_gt, ALU.mult) \
                      .then_inc(S[l].zsign_dve, 1)

            def mask_bits(l, T):
                if l == 0:
                    dve.wait_ge(cast_done, RGROUPS * (T.t + 1))
                else:
                    dve.wait_ge(mask_loaded[T.p], 16 * (T.n + 1))
                dve.wait_ge(S[l].zsign_act, 2 * (T.t + 1))
                dve.wait_ge(S[l].zsign_dve, 2 * (T.t + 1))
                bits = sign_z[:, T.p, :].bitcast(U32)
                nc.vector.scalar_tensor_tensor(out=bits, in0=bits, scalar=G2_WORD, in1=sign_a[:, T.p, :].bitcast(U32),
                                               op0=ALU.bitwise_xor, op1=ALU.bitwise_and).then_inc(S[l].edge_bits, 1)

            def turn_bits(l, T):
                dve.wait_ge(S[l].edge_bits, T.t + 1)
                if T.u is None and T.k < 2 and l:
                    dve.wait_ge(S[l - 1].tile_summed, TILES)
                T.wait_before(dve, S[l].tile_summed, 2)
                nc.vector.transpose(g2[:, T.p, :].bitcast(U32).rearrange("p (b r i) -> p r b i", r=RGROUPS, i=QROWS),
                                    sign_z[:, T.p, :].bitcast(U32).rearrange("p (r b i) -> p r b i", r=RGROUPS, i=QROWS)) \
                  .then_inc(S[l].turned, 1)

            def split_bits(l, T):
                dve.wait_ge(S[l].turned, T.t + 1)
                words = g2[:, T.p, :].bitcast(U32)
                nc.vector.tensor_scalar(g1[:, T.p, :].bitcast(U32), words, G1_WORD, None, ALU.bitwise_and) \
                  .then_inc(S[l].g1_ready, 1)
                dve.wait_ge(S[l].g1_ready, T.t + 1)
                nc.vector.tensor_scalar(words, words, 1, G1_WORD, ALU.logical_shift_left, ALU.bitwise_and) \
                  .then_inc(S[l].g_ready, 1)

            def finish_tile(l, T):
                p, fin = T.p, S[l].fin
                dve.wait_ge(S[l].part_a, T.t + 1)
                dve.wait_ge(S[l].tile_summed, T.t + 1)
                nc.vector.scalar_tensor_tensor(out=part_ac[:, p, :], in0=acc[p][1][:, 0:ROW], scalar=coef_c[:, ds(T.t, 1)],
                                               in1=part_a[:, p, :], op0=ALU.mult, op1=ALU.add).then_inc(S[l].part_ac, 1)
                dve.wait_ge(S[l].part_ac, T.t + 1)
                nc.vector.tensor_tensor(joined[:, p, :], part_ac[:, p, 0:PART], part_ac[:, p, PART:ROW], ALU.add).then_inc(fin, 1)
                dve.wait_ge(fin, FIN * T.t + 1)
                nc.vector.tensor_scalar(empty[:, p, :], joined[:, p, DIM:PART], 0.0, None, ALU.is_equal).then_inc(fin, 1)
                dve.wait_ge(fin, FIN * T.t + 2)
                nc.vector.tensor_tensor(den[:, p, :], joined[:, p, DIM:PART], empty[:, p, :], ALU.add).then_inc(fin, 1)
                nc.vector.scalar_tensor_tensor(out=numer[:, p, :], in0=h_mean[:], scalar=empty[:, p, :],
                                               in1=joined[:, p, 0:DIM], op0=ALU.mult, op1=ALU.add).then_inc(fin, 1)
                dve.wait_ge(fin, FIN * T.t + 3)
                nc.vector.reciprocal(rden[:, p, :], den[:, p, :]).then_inc(fin, 1)
                dve.wait_ge(fin, FIN * T.t + 5)
                dve.wait_ge(S[l].x_old[p], 16 * (T.n + 1))
                if T.u is not None or T.k >= 2:
                    dve.wait_ge(S[l].x_stored[p], 16 * T.n)
                elif l:
                    dve.wait_ge(S[0].x_stored[p], 16 * TILES // 2)
                if l == 0:
                    T.wait_before(dve, S[1].centred, 2)
                nc.vector.scalar_tensor_tensor(out=x_new[:, p, :], in0=numer[:, p, :], scalar=rden[:, p, :],
                                               in1=x_old[:, p, :], op0=ALU.mult, op1=ALU.add).then_inc(fin, 1)
                dve.wait_ge(fin, FIN * (T.t + 1))

            def open_layer(l):
                dve.wait_ge(S[l].mean_sum, TILES)
                nc.vector.tensor_copy(h_mean[:], ps_mean[:, 0:DIM]).then_inc(S[l].mean_kept, 1)
                dve.wait_ge(S[l].nat_ps, 1)
                if l:
                    dve.wait_ge(S[l - 1].nat_stored, 16)
                nc.vector.tensor_copy(nat_t[:], ps_t[0][:, 0:128]).then_inc(S[l].nat_sb, 1)
                dve.wait_ge(S[l].s_strip, 16 * QUADS)
                if l:
                    dve.wait_ge(S[l - 1].zsign_act, 2 * TILES)
                    dve.wait_ge(S[l - 1].zsign_dve, 2 * TILES)
                nc.vector.transpose(neg_s[:], s_strip[:]).then_inc(S[l].neg_s, 1)
                dve.wait_ge(S[l].neg_s, 1)
                dve.wait_ge(S[l].t_row, 16 * QUADS)
                dve.wait_ge(S[l].mean_kept, 1)
                dve.wait_ge(S[l].coefs, 2)

            def first_stats(T):
                if T.u is None and T.k % 8 == 0:
                    pass
                node_stats(0, T)

            def first_nodes(T):
                if T.u is None and T.k == 0:
                    first_stats(T)
                    first_stats(T.plus(1))
                if T.plus(2).exists:
                    first_stats(T.plus(2))
                node_ext(0, T)
                node_max(0, T)
                if T.plus(-1).exists:
                    node_low(0, T.plus(-1))

            dve.wait_ge(x_loaded, 16 * 8)
            sweep(dve, first_nodes)
            node_low(0, Tile(TILES - 1))

            def build_mask(l, T):
                z_sign(l, T)
                mask_bits(l, T)
                turn_bits(l, T)
                split_bits(l, T)

            for l in range(LAYERS):
                open_layer(l)
                build_mask(l, Tile(0))

                def tile(T):
                    done, ahead = T.plus(-1), T.plus(1)
                    if done.exists:
                        finish_tile(l, done)
                        if l == 0:
                            node_stats(1, done)
                    if ahead.exists:
                        z_sign(l, ahead)
                        mask_bits(l, ahead)
                        turn_bits(l, ahead)
                    if done.exists and l == 0:
                        node_ext(1, done)
                        node_max(1, done)
                    if ahead.exists:
                        split_bits(l, ahead)
                    if done.exists and l == 0:
                        node_low(1, done)

                sweep(dve, tile, trail=1)


_INS = ['x', 'adj', 'L0_gnn_W', 'L0_gnn_b_W', 'L0_gnn_a_vec', 'L0_gnn_b_a', 'L1_gnn_W_w', 'L1_gnn_W_b', 'L1_gnn_a']


def kernel(**inputs):
    import numpy as _np
    import concourse.bacc as _bacc
    from concourse import mybir as _mybir
    from concourse.bass_utils import run_bass_kernel_spmd as _run

    nc = _bacc.Bacc("TRN2", target_bir_lowering=False, num_devices=1)
    arrays, args = {}, []
    for name in _INS:
        a = _np.ascontiguousarray(inputs[name])
        arrays[f"in_{name}_dram"] = a
        args.append(nc.dram_tensor(f"in_{name}_dram", a.shape, _mybir.dt.from_np(a.dtype), kind="ExternalInput").ap())
    args.append(nc.dram_tensor("out_0_dram", (NODES, DIM), _mybir.dt.float32, kind="ExternalOutput").ap())
    gat_kernel(nc, *args)
    r = _run(nc, [arrays], core_ids=[0])
    return r.results[0]["out_0_dram"]
```

```python
import concourse.bass as bass
from concourse import mybir
from contextlib import ExitStack
import math

NODES = 8192
DIM = 128
LAYERS = 2
EPS = 1e-5
TILE = 128
TILES = NODES // TILE
QUADS = 4
QROWS = 32
SPAN = NODES // QUADS
RGROUPS = TILE // QROWS
BYTES = 4
BLOCKS = SPAN // (QROWS * BYTES)
CHUNKS = BLOCKS * BYTES
ONE = DIM
NEG_S, POS_T, LOG_B, LOG_D = DIM + 1, DIM + 2, DIM + 3, DIM + 4
EXT = DIM + 5
PART = DIM + 1
ROW = 2 * PART
KAPPA = 4.0
LEAK = 0.2
EDGE_WORD = 0x20202020
LOW_Z_WORD = 0x10101010
VGROUPS = 4
PER_GROUP = BLOCKS // VGROUPS
HEAD = 4
TAIL = 62
NODE_STEP = 4


class Tile:

    def __init__(self, k, u=None, step=2):
        self.k, self.u, self.step = k, u, step
        self.p, self.p4 = k % 2, k % 4
        self.t = k if u is None else step * u + k
        self.n = k // 2 if u is None else step // 2 * u + k // 2
        self.n4 = k // 4 if u is None else u + k // 4

    def plus(self, d):
        return Tile(self.k + d, self.u, self.step)

    @property
    def exists(self):
        return self.u is not None or 0 <= self.k < TILES

    def wait_before(self, eng, sem, back):
        if self.u is not None or self.k - back >= 0:
            eng.wait_ge(sem, self.t - back + 1)


def sweep(eng, body, trail=0, step=2):
    end = TILES - step
    for k in range(HEAD):
        body(Tile(k))
    with eng.Fori(HEAD // step, end // step) as u:
        for k in range(step):
            body(Tile(k, u, step))
    for k in range(end, TILES + trail):
        body(Tile(k))


def gat_kernel(nc, x, adj, w_0, b_w_0, a_vec_0, b_a_0, w_1, b_w_1, a_1, out):
    F32, F16, I8, I32, U32, FP8 = (mybir.dt.float32, mybir.dt.float16, mybir.dt.int8, mybir.dt.int32,
                                   mybir.dt.uint32, mybir.dt.float8e4)
    ALU, ACT, AX = mybir.AluOpType, mybir.ActivationFunctionType, mybir.AxisListType
    ds = bass.ds

    mask_dram = nc.dram_tensor("mask_bytes", (TILES, 128, NODES), I8, kind="Internal").ap()
    rows_dram = [nc.dram_tensor(f"node_rows_{l}", (TILES, TILE, 2 * ROW), F16, kind="Internal").ap() for l in range(LAYERS)]
    st_dram = [nc.dram_tensor(f"neg_s_and_t_{l}", (2, NODES), F32, kind="Internal").ap() for l in range(LAYERS)]
    x1_dram = nc.dram_tensor("x_after_layer_0", (NODES, DIM), F32, kind="Internal").ap()

    with ExitStack() as ctx:
        def sb(name, shape, dt):
            return ctx.enter_context(nc.sbuf_tensor(name, shape, dt))

        def ps(name):
            return ctx.enter_context(nc.psum_tensor(name, [128, 512], F32))

        def sem(name):
            return ctx.enter_context(nc.semaphore(name))

        adj_sb = sb("adj_sb", [128, RGROUPS, SPAN], I32)
        sign_a = sb("sign_a", [128, 2, NODES], I8)
        sign_z = sb("sign_z", [128, 2, NODES], I8)
        masks = sb("masks", [128, 2, 2, NODES], I8)
        g1, g2 = masks[:, 0, :, :], masks[:, 1, :, :]
        x_all = masks[:].rearrange("p m s c -> p (m s c)").bitcast(F32).rearrange("p (t d) -> p t d", d=DIM)
        t_row = sb("t_row", [128, SPAN], F32)
        node_rows = sb("node_rows", [128, CHUNKS, 2 * ROW], F16)
        nat = sb("nat", [128, 2 * TILES], F32)
        nat_t = sb("nat_t", [128, TILE], F32)
        s_strip = sb("s_strip", [128, TILES * RGROUPS], F32)
        neg_s = sb("neg_s", [128, TILES * RGROUPS], F32)
        coef_a = sb("coef_a", [128, TILES], F32)
        coef_c = sb("coef_c", [128, TILES], F32)
        h_sum = sb("h_sum", [128, DIM], F32)
        h_mean = sb("h_mean", [128, DIM], F32)
        part_a = sb("part_a", [128, 2, ROW], F32)
        part_ac = sb("part_ac", [128, 2, ROW], F32)
        joined = sb("joined", [128, 2, PART], F32)
        empty = sb("empty", [128, 2, 1], F32)
        den = sb("den", [128, 2, 1], F32)
        rden = sb("rden", [128, 2, 1], F32)
        numer = sb("numer", [128, 2, DIM], F32)
        x_old = sb("x_old", [128, 2, DIM], F32)
        x_new = sb("x_new", [128, 2, DIM], F32)
        stats = sb("stats", [128, 2, 6], F32)
        mean_var = sb("mean_var", [128, 2, 2], F32)
        var_eps = sb("var_eps", [128, 2, 1], F32)
        rstd = sb("rstd", [128, 2, 1], F32)
        centred = sb("centred", [128, 2, DIM], F32)
        centred_t = sb("centred_t", [128, 2, DIM], F32)
        ext = sb("ext", [128, 2, EXT], F32)
        b_and_d = sb("b_and_d", [128, 2, 2], F32)
        row_parts = sb("row_parts", [128, 4, 2 * ROW], F16)
        ident = sb("ident", [128, 128], F32)
        averager = sb("averager", [128, 128], F32)
        minus_half = sb("minus_half", [128, 1], F32)
        w_raw = [sb(f"w_raw_{l}", [128, 128], F32) for l in range(LAYERS)]
        w_tr = [sb(f"w_tr_{l}", [128, 128], F32) for l in range(LAYERS)]
        a_raw = [sb(f"a_raw_{l}", [128, 2], F32) for l in range(LAYERS)]
        b_raw = [sb(f"b_raw_{l}", [128, 1], F32) for l in range(LAYERS)]
        b_a_sb = sb("b_a_sb", [128, 1], F32)
        b_wide = [sb(f"b_wide_{l}", [128, 128], F32) for l in range(LAYERS)]
        id_and_a = [sb(f"id_and_a_{l}", [128, EXT], F32) for l in range(LAYERS)]
        w_ext = [sb(f"w_ext_{l}", [128, EXT], F32) for l in range(LAYERS)]
        bias = [sb(f"bias_{l}", [128, EXT], F32) for l in range(LAYERS)]

        acc = [[ps(f"acc_{p}_{s}") for s in range(2)] for p in range(2)]
        ps_t = [ps(f"ps_t_{p}") for p in range(2)]
        ps_h = ps("ps_h")
        ps_mean = ps("ps_mean")

        weights_loaded, ident_ready = sem("weights_loaded"), sem("ident_ready")
        setup_pe, setup_dve = sem("setup_pe"), sem("setup_dve")
        x_head, x_rest, rows_free = sem("x_head"), sem("x_rest"), sem("rows_free")
        adj_loaded = [sem(f"adj_loaded_{r}") for r in range(RGROUPS)]
        cast_done = sem("cast_done")
        mask_stored = [sem(f"mask_stored_{p}") for p in range(2)]
        mask_loaded = [sem(f"mask_loaded_{p}") for p in range(2)]

        class LayerSems:
            def __init__(self, l):
                self.zsign_act, self.zsign_dve = sem(f"zsign_act_{l}"), sem(f"zsign_dve_{l}")
                self.edge_bits, self.turned = sem(f"edge_bits_{l}"), sem(f"turned_{l}")
                self.g1_ready, self.g_ready = sem(f"g1_ready_{l}"), sem(f"g_ready_{l}")
                self.tile_summed = sem(f"tile_summed_{l}")
                self.part_a, self.part_ac, self.fin = sem(f"part_a_{l}"), sem(f"part_ac_{l}"), sem(f"fin_{l}")
                self.x_old = [sem(f"x_old_{l}_{p}") for p in range(2)]
                self.x_stored = [sem(f"x_stored_{l}_{p}") for p in range(2)]
                self.stats, self.mean_var = sem(f"stats_{l}"), sem(f"mean_var_{l}")
                self.centred, self.var_eps, self.rstd = sem(f"centred_{l}"), sem(f"var_eps_{l}"), sem(f"rstd_{l}")
                self.turned_ps, self.centred_t = sem(f"turned_ps_{l}"), sem(f"centred_t_{l}")
                self.h_raw, self.ext = sem(f"h_raw_{l}"), sem(f"ext_{l}")
                self.h_sum, self.h_mean, self.st_kept = sem(f"h_sum_{l}"), sem(f"h_mean_{l}"), sem(f"st_kept_{l}")
                self.b_and_d, self.high_b, self.high_d, self.low = \
                    sem(f"b_and_d_{l}"), sem(f"high_b_{l}"), sem(f"high_d_{l}"), sem(f"low_{l}")
                self.rows_stored = [sem(f"rows_stored_{l}_{p}") for p in range(4 - 2 * l)]
                self.nat_ps, self.nat_sb, self.nat_stored = sem(f"nat_ps_{l}"), sem(f"nat_sb_{l}"), sem(f"nat_stored_{l}")
                self.t_row, self.s_strip = sem(f"t_row_{l}"), sem(f"s_strip_{l}")
                self.neg_s, self.mean_kept, self.coefs = sem(f"neg_s_{l}"), sem(f"mean_kept_{l}"), sem(f"coefs_{l}")
                self.rows_loaded = [sem(f"rows_loaded_{l}_{g}") for g in range(VGROUPS)]

        S = [LayerSems(l) for l in range(LAYERS)]
        x_src = [x, x1_dram]
        x_dst = [x1_dram, out]

        def row_slot(l, T):
            return (T.p4, T.n4) if l == 0 else (T.p, T.n)

        FIN = 6

        def x_of(l, T):
            return x_all[:, ds(T.t, 1), :].rearrange("p o d -> p (o d)") if l == 0 else x_new[:, T.p, :]

        block = ctx.enter_context(nc.Block())

        @block.sync
        def _(sp):
            def load_adj(T, r):
                for a in range(QUADS):
                    sp.nop(nofuse=True)
                    sp.dma_start(adj_sb[QROWS * a:QROWS * (a + 1), r, :],
                                 adj[ds(T.t * TILE + QROWS * r, QROWS), SPAN * a:SPAN * (a + 1)]) \
                      .then_inc(adj_loaded[r], 16)

            def load_x_old(l, T):
                if T.u is not None or T.k >= 2:
                    sp.wait_ge(S[l].fin, FIN * (T.t - 1))
                sp.nop(nofuse=True)
                sp.dma_start(x_old[:, T.p, :], x_src[l][ds(T.t * TILE, TILE), :]).then_inc(S[l].x_old[T.p], 16)

            def store_x_new(l, T):
                sp.wait_ge(S[l].fin, FIN * (T.t + 1))
                sp.nop(nofuse=True)
                sp.dma_start(x_dst[l][ds(T.t * TILE, TILE), :], x_new[:, T.p, :]).then_inc(S[l].x_stored[T.p], 16)

            def store_rows(l, T):
                sp.wait_ge(S[l].low, T.t + 1)
                sp.nop(nofuse=True)
                slot, _ = row_slot(l, T)
                sp.dma_start(rows_dram[l][ds(T.t, 1), :, :].rearrange("o p r -> p (o r)"), row_parts[:, slot, :]) \
                  .then_inc(S[l].rows_stored[slot], 16)

            def spread_layer(l):
                sp.wait_ge(S[l].nat_sb, 1)
                sp.dma_start(st_dram[l].rearrange("c (t m) -> (c t) m", m=TILE), nat_t[:]).then_inc(S[l].nat_stored, 16)
                sp.wait_ge(S[l].nat_stored, 16)
                if l:
                    sp.wait_ge(S[l - 1].zsign_dve, 2 * TILES)
                    sp.wait_ge(S[l - 1].zsign_act, 2 * TILES)
                for a in range(QUADS):
                    quad = slice(QROWS * a, QROWS * (a + 1))
                    sp.dma_start(s_strip[quad, :].rearrange("p (g i) -> p g i", i=QROWS),
                                 st_dram[l][0, :].rearrange("(g p i) -> p g i", p=QROWS, i=QROWS)).then_inc(S[l].s_strip, 16)
                    sp.dma_start(t_row[quad, :],
                                 st_dram[l][1, SPAN * a:SPAN * (a + 1)].partition_broadcast(QROWS)).then_inc(S[l].t_row, 16)

            def load_rows(l, a, g):
                src = rows_dram[l][BLOCKS * a + PER_GROUP * g:BLOCKS * a + PER_GROUP * (g + 1), :, :]
                dst = node_rows[QROWS * a:QROWS * (a + 1), BYTES * PER_GROUP * g:BYTES * PER_GROUP * (g + 1), :]
                sp.dma_start(dst.rearrange("p (b k) r -> p b (k r)", k=BYTES),
                             src.rearrange("b (j k) r -> j b (k r)", k=BYTES)).then_inc(S[l].rows_loaded[g], 16)

            sp.dma_start(w_raw[0][:], w_0).then_inc(weights_loaded, 16)
            sp.dma_start(w_raw[1][:], w_1).then_inc(weights_loaded, 16)
            with nc.allow_non_contiguous_dma(reason="weight vectors onto partitions, once"):
                sp.dma_start(a_raw[0][:], a_vec_0.rearrange("(c p) -> p c", p=DIM)).then_inc(weights_loaded, 16)
                sp.dma_start(a_raw[1][:], a_1.rearrange("(c p) o -> p (c o)", p=DIM)).then_inc(weights_loaded, 16)
                sp.dma_start(b_raw[0][:], b_w_0.rearrange("(p o) -> p o", o=1)).then_inc(weights_loaded, 16)
                sp.dma_start(b_raw[1][:], b_w_1.rearrange("(p o) -> p o", o=1)).then_inc(weights_loaded, 16)
                sp.dma_start(b_a_sb[:], b_a_0.partition_broadcast(128)).then_inc(weights_loaded, 16)
            x_tiles = x.rearrange("(t m) d -> m t d", m=TILE)
            first = 8
            sp.dma_start(x_all[:, 0:first, :], x_tiles[:, 0:first, :]).then_inc(x_head, 16)
            for g in range(1, TILES // first):
                sp.dma_start(x_all[:, first * g:first * (g + 1), :], x_tiles[:, first * g:first * (g + 1), :]).then_inc(x_rest, 16)
            for r in range(RGROUPS):
                load_adj(Tile(0), r)
            def load_quadrant(a):
                for p in range(4):
                    sp.wait_ge(S[0].rows_stored[p], 16 * BLOCKS // 4 * (a + 1))
                for g in range(VGROUPS):
                    load_rows(0, a, g)

            for a in range(QUADS):
                for k in range(BLOCKS * a, BLOCKS * a + NODE_STEP):
                    store_rows(0, Tile(k))
                if a:
                    load_quadrant(a - 1)
                with sp.Fori(BLOCKS // NODE_STEP * a + 1, BLOCKS // NODE_STEP * (a + 1)) as u:
                    for k in range(NODE_STEP):
                        store_rows(0, Tile(k, u, NODE_STEP))
            spread_layer(0)
            load_quadrant(QUADS - 1)

            load_x_old(0, Tile(0))
            load_x_old(0, Tile(1))

            def store_mask(T):
                sp.wait_ge(cast_done, RGROUPS * (T.t + 1))
                sp.nop(nofuse=True)
                sp.dma_start(mask_dram[ds(T.t, 1), :, :].rearrange("o p c -> p (o c)"), sign_a[:, T.p, :]) \
                  .then_inc(mask_stored[T.p], 16)

            def load_mask(T):
                T.wait_before(sp, S[1].edge_bits, 2)
                sp.nop(nofuse=True)
                sp.dma_start(sign_a[:, T.p, :], mask_dram[ds(T.t, 1), :, :].rearrange("o p c -> p (o c)")) \
                  .then_inc(mask_loaded[T.p], 16)

            def layer_0_tile(T):
                if T.plus(1).exists:
                    for r in range(RGROUPS):
                        sp.wait_ge(cast_done, RGROUPS * T.t + r + 1)
                        load_adj(T.plus(1), r)
                store_mask(T)
                if T.plus(-3).exists:
                    store_x_new(0, T.plus(-3))
                    load_x_old(0, T.plus(-1))
                    store_rows(1, T.plus(-3))

            sweep(sp, layer_0_tile)
            load_x_old(0, Tile(TILES - 1))
            for k in range(TILES - 3, TILES):
                store_x_new(0, Tile(k))
                store_rows(1, Tile(k))
                if k == TILES - 2:
                    sp.wait_ge(S[0].edge_bits, TILES)
                    for p in range(2):
                        sp.wait_ge(mask_stored[p], 16 * TILES // 2)
                        load_mask(Tile(p))
                if k == TILES - 3:
                    for p in range(2):
                        sp.wait_ge(S[1].rows_stored[p], 16 * (TILES // 2 - PER_GROUP // 2))
                for g in [[0], [1, 2, 3], []][k - (TILES - 3)]:
                    if g < VGROUPS - 1:
                        sp.wait_ge(rows_free, g + 1)
                    else:
                        sp.wait_ge(S[0].tile_summed, TILES)
                    for a in range(QUADS):
                        if (a, g) != (QUADS - 1, VGROUPS - 1):
                            load_rows(1, a, g)

            spread_layer(1)
            for p in range(2):
                sp.wait_ge(S[1].rows_stored[p], 16 * TILES // 2)
            load_rows(1, QUADS - 1, VGROUPS - 1)
            for p in range(2):
                sp.wait_ge(S[0].x_stored[p], 16 * TILES // 2)
            load_x_old(1, Tile(0))
            load_x_old(1, Tile(1))

            def layer_1_tile(T):
                if T.plus(2).exists:
                    load_mask(T.plus(2))
                if T.plus(-2).exists:
                    store_x_new(1, T.plus(-2))
                    load_x_old(1, T)

            for k in range(HEAD):
                layer_1_tile(Tile(k))
            with sp.Fori(HEAD // 2, TAIL // 2) as u:
                for k in range(2):
                    layer_1_tile(Tile(k, u))
            for k in range(TAIL, TILES):
                layer_1_tile(Tile(k))
            store_x_new(1, Tile(TILES - 2))
            store_x_new(1, Tile(TILES - 1))
            for p in range(2):
                sp.wait_ge(S[1].x_stored[p], 16 * TILES // 2)

        @block.gpsimd
        def _(pool):
            pool.memset(minus_half[:], -0.5).then_inc(ident_ready, 1)
            pool.memset(averager[:], 1.0 / NODES).then_inc(ident_ready, 1)
            pool.memset(ident[:], 0.0).then_inc(ident_ready, 1)
            pool.wait_ge(ident_ready, 3)
            pool.affine_select(out=ident[:], in_=ident[:], compare_op=ALU.not_equal, fill=1.0, base=0,
                               pattern=[[-1, 128]], channel_multiplier=1).then_inc(ident_ready, 1)

            nat_v = nat[:].rearrange("p (c t) -> p c t", c=2)

            def node_step(l, T):
                pool.wait_ge(S[l].var_eps, T.t + 1)
                T.wait_before(pool, S[l].ext, 2)
                pool.nop(nofuse=True)
                pool.tensor_tensor(rstd[:, T.p, :], var_eps[:, T.p, :], minus_half[:], ALU.pow).then_inc(S[l].rstd, 1)

            def node_rest(l, T):
                pool.wait_ge(S[l].ext, T.t + 1)
                if T.u is None and T.k == 0:
                    if l:
                        pool.wait_ge(S[0].h_mean, 1)
                    pool.tensor_copy(h_sum[:], ext[:, T.p, 0:DIM]).then_inc(S[l].h_sum, 1)
                else:
                    pool.wait_ge(S[l].h_sum, T.t)
                    pool.nop(nofuse=True)
                    pool.tensor_tensor(h_sum[:], h_sum[:], ext[:, T.p, 0:DIM], ALU.add).then_inc(S[l].h_sum, 1)
                pool.tensor_copy(nat_v[:, :, ds(T.t, 1)], ext[:, T.p, NEG_S:POS_T + 1].rearrange("p (c o) -> p c o", o=1)) \
                    .then_inc(S[l].st_kept, 1)
                pool.wait_ge(S[l].b_and_d, T.t + 1)
                slot, used = row_slot(l, T)
                if T.u is not None or used:
                    pool.wait_ge(S[l].rows_stored[slot], 16 * used)
                pool.nop(nofuse=True)
                pool.tensor_scalar(row_parts[:, slot, ROW:ROW + PART], ext[:, T.p, 0:PART], b_and_d[:, T.p, 1:2], 1.0,
                                   ALU.mult, ALU.mult).then_inc(S[l].high_d, 1)

            for l in range(LAYERS):
                if l:
                    pool.wait_ge(S[0].nat_ps, 1)
                    pool.wait_ge(S[0].coefs, 2)

                def body(T):
                    if T.exists:
                        node_step(l, T)
                    rest = T.plus(l - 1)
                    if rest.exists:
                        node_rest(l, rest)

                sweep(pool, body, trail=1 - l, step=[NODE_STEP, 2][l])

        @block.tensor
        def _(pe):
            pe.wait_ge(weights_loaded, 7 * 16)
            pe.wait_ge(ident_ready, 4)
            for l in range(LAYERS):
                pe.transpose(ps_t[l][:, 0:128], w_raw[l][:], ident[:]).then_inc(setup_pe, 1)
            pe.wait_ge(setup_dve, LAYERS)
            w_oi = [w_raw[0], w_tr[1]]
            for l in range(LAYERS):
                pe.matmul(ps_h[:, 8 * l:8 * l + 5], w_oi[l][:], id_and_a[l][:, DIM:EXT], start=True, stop=True) \
                  .then_inc(setup_pe, 1)
                pe.matmul(acc[0][l][:, 0:EXT], b_wide[l][:], id_and_a[l][:], start=True, stop=True).then_inc(setup_pe, 1)
            pe.wait_ge(setup_dve, 2 * LAYERS)

            def turn(l, T):
                pe.wait_ge(S[l].centred, T.t + 1)
                T.wait_before(pe, S[l].centred_t, 2)
                pe.transpose(ps_t[T.p][:, 0:DIM], centred[:, T.p, :], ident[:]).then_inc(S[l].turned_ps, 1)

            def project(l, T):
                pe.wait_ge(S[l].centred_t, T.t + 1)
                T.wait_before(pe, S[l].ext, 1)
                pe.matmul(ps_h[:, 0:EXT], centred_t[:, T.p, :], w_ext[l][:], start=True, stop=True).then_inc(S[l].h_raw, 1)

            def close_nodes(l):
                pe.wait_ge(S[l].st_kept, TILES)
                pe.wait_ge(S[l].centred_t, TILES)
                pe.transpose(ps_t[0][:, 0:128], nat[:], ident[:]).then_inc(S[l].nat_ps, 1)
                pe.wait_ge(S[l].h_sum, TILES)
                pe.matmul(ps_mean[:, 0:DIM], averager[:], h_sum[:], start=True, stop=True).then_inc(S[l].h_mean, 1)

            def first_nodes(T):
                if T.u is None and T.k == 0:
                    turn(0, T)
                if T.plus(1).exists:
                    turn(0, T.plus(1))
                project(0, T)

            sweep(pe, first_nodes, step=NODE_STEP)
            close_nodes(0)

            turn_at, project_at = 20, 34

            for l in range(LAYERS):
                def tile(T):
                    pe.wait_ge(S[l].g_ready, T.t + 1)
                    T.wait_before(pe, S[l].part_a, 2)
                    T.wait_before(pe, S[l].part_ac, 2)
                    pe.nop(nofuse=True)
                    stationary = [m[:, T.p, :].bitcast(FP8).rearrange("p (b i k) -> p b k i", b=BLOCKS, k=BYTES)
                                  for m in (g1, g2)]
                    for c in range(CHUNKS):
                        if T.u is None and T.k == 0 and c % (CHUNKS // VGROUPS) == 0:
                            pe.wait_ge(S[l].rows_loaded[c // (CHUNKS // VGROUPS)], 16 * QUADS)
                        for s in range(2):
                            mm = pe.matmul(acc[T.p][s][:, 0:ROW], stationary[s][:, c // BYTES, c % BYTES, :],
                                           node_rows[:, c, ROW * s:ROW * (s + 1)],
                                           start=(c == 0), stop=(c == CHUNKS - 1), skip_group_check=True)
                        if l == 0 and T.u is None and T.k == TILES - 1 and c % (CHUNKS // VGROUPS) == CHUNKS // VGROUPS - 1 \
                                and c < CHUNKS - 1:
                            mm.then_inc(rows_free, 1)
                        if l == 0 and T.plus(-1).exists:
                            if c == turn_at:
                                turn(1, T.plus(-1))
                            if c == project_at:
                                project(1, T.plus(-1))
                    mm.then_inc(S[l].tile_summed, 1)

                if l == 0:
                    pe.wait_ge(S[0].mean_kept, 1)
                    pe.wait_ge(S[0].nat_sb, 1)
                sweep(pe, tile)
                if l == 0:
                    last = Tile(TILES - 1)
                    turn(1, last)
                    project(1, last)
                    close_nodes(1)

        @block.scalar
        def _(act):
            def node_copy(l, T):
                act.wait_ge(S[l].turned_ps, T.t + 1)
                T.wait_before(act, S[l].h_raw, 2)
                nc.scalar.copy(centred_t[:, T.p, :], ps_t[T.p][:, 0:DIM]).then_inc(S[l].centred_t, 1)

            def node_high(l, T):
                act.wait_ge(S[l].ext, T.t + 1)
                T.wait_before(act, S[l].high_b, 2)
                T.wait_before(act, S[l].low, 2)
                slot, used = row_slot(l, T)
                if T.u is not None or used:
                    act.wait_ge(S[l].rows_stored[slot], 16 * used)
                nc.scalar.activation(b_and_d[:, T.p, :], ext[:, T.p, LOG_B:LOG_D + 1], ACT.Exp).then_inc(S[l].b_and_d, 1)
                act.wait_ge(S[l].b_and_d, T.t + 1)
                nc.scalar.activation(row_parts[:, slot, 0:PART], ext[:, T.p, 0:PART], ACT.Copy, scale=b_and_d[:, T.p, 0:1]) \
                  .then_inc(S[l].high_b, 1)

            def cast(T, r):
                if r == 0 and (T.u is not None or T.k >= 2):
                    act.wait_ge(S[0].edge_bits, T.t - 1)
                    act.wait_ge(mask_stored[T.p], 16 * T.n)
                act.wait_ge(adj_loaded[r], 16 * QUADS * (T.t + 1))
                nc.scalar.activation(sign_a[:, T.p, SPAN * r:SPAN * (r + 1)], adj_sb[:, r, :], ACT.Sign, scale=-1.0) \
                  .then_inc(cast_done, 1)

            def z_sign(l, T, r):
                if r == 0:
                    T.wait_before(act, S[l].turned, 2)
                nc.scalar.activation(sign_z[:, T.p, SPAN * r:SPAN * (r + 1)], t_row[:], ACT.Sign, scale=-1.0,
                                     bias=neg_s[:, ds(RGROUPS * T.t + r, 1)]).then_inc(S[l].zsign_act, 1)

            def part_one(l, T):
                act.wait_ge(S[l].tile_summed, T.t + 1)
                T.wait_before(act, S[l].part_ac, 2)
                nc.scalar.activation(part_a[:, T.p, :], acc[T.p][0][:, 0:ROW], ACT.Copy, scale=coef_a[:, ds(T.t, 1)]) \
                  .then_inc(S[l].part_a, 1)

            def open_layer(l):
                act.wait_ge(S[l].st_kept, TILES)
                if l:
                    act.wait_ge(S[l - 1].part_ac, TILES)
                    act.wait_ge(S[l - 1].part_a, TILES)
                nc.scalar.activation(coef_a[:], nat[:, 0:TILES], ACT.Exp, scale=-1.0).then_inc(S[l].coefs, 1)
                nc.scalar.activation(coef_c[:], nat[:, 0:TILES], ACT.Exp, scale=-LEAK).then_inc(S[l].coefs, 1)

            def first_nodes(T):
                if T.u is None and T.k == 0:
                    node_copy(0, T)
                if T.plus(1).exists:
                    node_copy(0, T.plus(1))
                node_high(0, T)
                if T.u is None and T.k < RGROUPS:
                    cast(Tile(0), T.k)

            sweep(act, first_nodes, step=NODE_STEP)
            open_layer(0)
            cast(Tile(1), 0)
            cast(Tile(1), 1)
            act.wait_ge(S[0].neg_s, 1)
            act.wait_ge(S[0].t_row, 16 * QUADS)
            act.wait_ge(S[0].coefs, 2)
            for r in range(2):
                z_sign(0, Tile(0), r)
            cast(Tile(1), 2)
            cast(Tile(1), 3)
            for r in range(2):
                z_sign(0, Tile(1), r)

            def layer_0_tile(T):
                done, ahead = T.plus(-1), T.plus(2)
                if done.exists:
                    part_one(0, done)
                if ahead.exists:
                    cast(ahead, 0)
                    cast(ahead, 1)
                if done.exists:
                    node_copy(1, done)
                if ahead.exists:
                    cast(ahead, 2)
                    cast(ahead, 3)
                    z_sign(0, ahead, 0)
                if done.exists:
                    node_high(1, done)
                if ahead.exists:
                    z_sign(0, ahead, 1)

            sweep(act, layer_0_tile, trail=1)
            open_layer(1)
            act.wait_ge(S[1].neg_s, 1)
            act.wait_ge(S[1].t_row, 16 * QUADS)
            act.wait_ge(S[1].coefs, 2)
            act.wait_ge(S[0].turned, TILES)
            for k in range(2):
                for r in range(2):
                    z_sign(1, Tile(k), r)

            def layer_1_tile(T):
                if T.plus(-1).exists:
                    part_one(1, T.plus(-1))
                if T.plus(2).exists:
                    for r in range(2):
                        z_sign(1, T.plus(2), r)

            sweep(act, layer_1_tile, trail=1)

        @block.vector
        def _(dve):
            dve.wait_ge(weights_loaded, 7 * 16)
            dve.wait_ge(ident_ready, 4)
            steps = sem("setup_steps")
            n_steps = [0]

            def step(ins):
                n_steps[0] += 1
                ins.then_inc(steps, 1)
                dve.wait_ge(steps, n_steps[0])

            for l in range(LAYERS):
                ia = id_and_a[l]
                step(nc.vector.tensor_copy(ia[:, 0:DIM], ident[:]))
                step(nc.vector.memset(ia[:, ONE:ONE + 1], 0.0))
                step(nc.vector.tensor_scalar(ia[:, NEG_S:NEG_S + 1], a_raw[l][:, 0:1], -1.0, None, ALU.mult))
                step(nc.vector.tensor_copy(ia[:, POS_T:POS_T + 1], a_raw[l][:, 1:2]))
                step(nc.vector.tensor_copy(ia[:, LOG_B:LOG_B + 1], a_raw[l][:, 1:2]))
                step(nc.vector.tensor_scalar(ia[:, LOG_D:LOG_D + 1], a_raw[l][:, 1:2], LEAK, None, ALU.mult))
                step(nc.vector.tensor_scalar(b_wide[l][:], ident[:], 0.0, b_raw[l][:, 0:1], ALU.mult, ALU.add))
                dve.wait_ge(setup_pe, l + 1)
                nc.vector.tensor_copy(w_tr[l][:], ps_t[l][:, 0:128]).then_inc(setup_dve, 1)
            dve.wait_ge(setup_dve, LAYERS)
            w_io = [w_tr[0], w_raw[1]]
            for l in range(LAYERS):
                dve.wait_ge(setup_pe, 3 * LAYERS)
                step(nc.vector.tensor_copy(w_ext[l][:, 0:DIM], w_io[l][:]))
                step(nc.vector.tensor_copy(w_ext[l][:, DIM:EXT], ps_h[:, 8 * l:8 * l + 5]))
                step(nc.vector.tensor_copy(bias[l][:], acc[0][l][:, 0:EXT]))
                step(nc.vector.tensor_scalar(bias[l][:, ONE:ONE + 1], bias[l][:, ONE:ONE + 1], 1.0, None, ALU.add))
                if l == 0:
                    step(nc.vector.tensor_tensor(bias[0][:, NEG_S:NEG_S + 1], bias[0][:, NEG_S:NEG_S + 1], b_a_sb[:],
                                                 ALU.subtract))
                nc.vector.tensor_scalar(bias[l][:, LOG_B:EXT], bias[l][:, LOG_B:EXT], math.log(KAPPA), None, ALU.add) \
                  .then_inc(setup_dve, 1)
            dve.wait_ge(setup_dve, 2 * LAYERS)

            def node_stats(l, T):
                T.wait_before(dve, S[l].mean_var, 2)
                nc.vector.bn_stats(stats[:, T.p, :], x_of(l, T)).then_inc(S[l].stats, 1)

            def node_mean(l, T):
                dve.wait_ge(S[l].stats, T.t + 1)
                T.wait_before(dve, S[l].centred, 2)
                T.wait_before(dve, S[l].var_eps, 2)
                dve.nop(nofuse=True)
                nc.vector.bn_aggr(mean_var[:, T.p, :], stats[:, T.p, :]).then_inc(S[l].mean_var, 1)

            def node_centre(l, T):
                dve.wait_ge(S[l].mean_var, T.t + 1)
                T.wait_before(dve, S[l].turned_ps, 2)
                nc.vector.tensor_scalar(centred[:, T.p, :], x_of(l, T), mean_var[:, T.p, 0:1], 0.0, ALU.subtract, ALU.max) \
                    .then_inc(S[l].centred, 1)
                T.wait_before(dve, S[l].rstd, 2)
                nc.vector.tensor_scalar(var_eps[:, T.p, :], mean_var[:, T.p, 1:2], EPS, None, ALU.add) \
                    .then_inc(S[l].var_eps, 1)

            def node_ext(l, T):
                dve.wait_ge(S[l].h_raw, T.t + 1)
                dve.wait_ge(S[l].rstd, T.t + 1)
                T.wait_before(dve, S[l].high_b, 2)
                T.wait_before(dve, S[l].high_d, 2)
                T.wait_before(dve, S[l].h_sum, 2)
                T.wait_before(dve, S[l].st_kept, 2)
                T.wait_before(dve, S[l].low, 2)
                nc.vector.scalar_tensor_tensor(out=ext[:, T.p, :], in0=ps_h[:, 0:EXT], scalar=rstd[:, T.p, 0:1],
                                               in1=bias[l][:], op0=ALU.mult, op1=ALU.add).then_inc(S[l].ext, 1)

            def node_low(l, T, s):
                dve.wait_ge([S[l].high_b, S[l].high_d][s], T.t + 1)
                slot, _ = row_slot(l, T)
                ins = nc.vector.scalar_tensor_tensor(
                    out=row_parts[:, slot, ROW * s + PART:ROW * (s + 1)], in0=ext[:, T.p, 0:PART],
                    scalar=b_and_d[:, T.p, s:s + 1], in1=row_parts[:, slot, ROW * s:ROW * s + PART],
                    op0=ALU.mult, op1=ALU.subtract)
                if s == 1:
                    ins.then_inc(S[l].low, 1)

            def z_sign(l, T):
                if T.u is None and T.k < 2 and l:
                    dve.wait_ge(S[l - 1].turned, TILES)
                T.wait_before(dve, S[l].turned, 2)
                for r in range(2, RGROUPS):
                    nc.vector.tensor_scalar(sign_z[:, T.p, SPAN * r:SPAN * (r + 1)], t_row[:],
                                            neg_s[:, ds(RGROUPS * T.t + r, 1)], -1.0, ALU.is_gt, ALU.mult) \
                      .then_inc(S[l].zsign_dve, 1)

            def mask_bits(l, T):
                if l == 0:
                    dve.wait_ge(cast_done, RGROUPS * (T.t + 1))
                else:
                    dve.wait_ge(mask_loaded[T.p], 16 * (T.n + 1))
                dve.wait_ge(S[l].zsign_act, 2 * (T.t + 1))
                dve.wait_ge(S[l].zsign_dve, 2 * (T.t + 1))
                bits = sign_z[:, T.p, :].bitcast(U32)
                nc.vector.scalar_tensor_tensor(out=bits, in0=bits, scalar=LOW_Z_WORD, in1=sign_a[:, T.p, :].bitcast(U32),
                                               op0=ALU.bitwise_xor, op1=ALU.bitwise_and).then_inc(S[l].edge_bits, 1)

            def turn_bits(l, T):
                dve.wait_ge(S[l].edge_bits, T.t + 1)
                if T.u is None and T.k < 2 and l:
                    dve.wait_ge(S[l - 1].tile_summed, TILES)
                T.wait_before(dve, S[l].tile_summed, 2)
                nc.vector.transpose(g2[:, T.p, :].bitcast(U32).rearrange("p (b r i) -> p r b i", r=RGROUPS, i=QROWS),
                                    sign_z[:, T.p, :].bitcast(U32).rearrange("p (r b i) -> p r b i", r=RGROUPS, i=QROWS)) \
                  .then_inc(S[l].turned, 1)

            def split_bits(l, T):
                dve.wait_ge(S[l].turned, T.t + 1)
                words = g2[:, T.p, :].bitcast(U32)
                nc.vector.tensor_scalar(g1[:, T.p, :].bitcast(U32), words, EDGE_WORD, None, ALU.bitwise_and).then_inc(S[l].g1_ready, 1)
                dve.wait_ge(S[l].g1_ready, T.t + 1)
                nc.vector.tensor_scalar(words, words, 1, EDGE_WORD,
                                        ALU.logical_shift_left, ALU.bitwise_and).then_inc(S[l].g_ready, 1)

            def finish_tile(l, T):
                p, fin = T.p, S[l].fin
                dve.wait_ge(S[l].part_a, T.t + 1)
                dve.wait_ge(S[l].tile_summed, T.t + 1)
                nc.vector.scalar_tensor_tensor(out=part_ac[:, p, :], in0=acc[p][1][:, 0:ROW], scalar=coef_c[:, ds(T.t, 1)],
                                               in1=part_a[:, p, :], op0=ALU.mult, op1=ALU.add).then_inc(S[l].part_ac, 1)
                dve.wait_ge(S[l].part_ac, T.t + 1)
                nc.vector.tensor_tensor(joined[:, p, :], part_ac[:, p, 0:PART], part_ac[:, p, PART:ROW], ALU.add).then_inc(fin, 1)
                dve.wait_ge(fin, FIN * T.t + 1)
                nc.vector.tensor_scalar(empty[:, p, :], joined[:, p, DIM:PART], 0.0, None, ALU.is_equal).then_inc(fin, 1)
                dve.wait_ge(fin, FIN * T.t + 2)
                nc.vector.tensor_tensor(den[:, p, :], joined[:, p, DIM:PART], empty[:, p, :], ALU.add).then_inc(fin, 1)
                nc.vector.scalar_tensor_tensor(out=numer[:, p, :], in0=h_mean[:], scalar=empty[:, p, :],
                                               in1=joined[:, p, 0:DIM], op0=ALU.mult, op1=ALU.add).then_inc(fin, 1)
                dve.wait_ge(fin, FIN * T.t + 3)
                nc.vector.reciprocal(rden[:, p, :], den[:, p, :]).then_inc(fin, 1)
                dve.wait_ge(fin, FIN * T.t + 5)
                dve.wait_ge(S[l].x_old[p], 16 * (T.n + 1))
                if T.u is not None or T.k >= 2:
                    dve.wait_ge(S[l].x_stored[p], 16 * T.n)
                elif l:
                    dve.wait_ge(S[0].x_stored[p], 16 * TILES // 2)
                if l == 0:
                    T.wait_before(dve, S[1].centred, 2)
                nc.vector.scalar_tensor_tensor(out=x_new[:, p, :], in0=numer[:, p, :], scalar=rden[:, p, :],
                                               in1=x_old[:, p, :], op0=ALU.mult, op1=ALU.add).then_inc(fin, 1)
                dve.wait_ge(fin, FIN * (T.t + 1))

            def open_layer(l):
                dve.wait_ge(S[l].h_mean, 1)
                nc.vector.tensor_copy(h_mean[:], ps_mean[:, 0:DIM]).then_inc(S[l].mean_kept, 1)
                dve.wait_ge(S[l].nat_ps, 1)
                if l:
                    dve.wait_ge(S[l - 1].nat_stored, 16)
                nc.vector.tensor_copy(nat_t[:], ps_t[0][:, 0:128]).then_inc(S[l].nat_sb, 1)
                dve.wait_ge(S[l].s_strip, 16 * QUADS)
                if l:
                    dve.wait_ge(S[l - 1].zsign_act, 2 * TILES)
                    dve.wait_ge(S[l - 1].zsign_dve, 2 * TILES)
                nc.vector.transpose(neg_s[:], s_strip[:]).then_inc(S[l].neg_s, 1)
                dve.wait_ge(S[l].neg_s, 1)
                dve.wait_ge(S[l].t_row, 16 * QUADS)
                dve.wait_ge(S[l].mean_kept, 1)
                dve.wait_ge(S[l].coefs, 2)

            def first_nodes(T):
                if T.u is None and T.k == 0:
                    for k in range(2):
                        node_stats(0, Tile(k))
                        node_mean(0, Tile(k))
                        node_centre(0, Tile(k))
                if T.u is None and T.k == HEAD - 1:
                    dve.wait_ge(x_rest, 16 * (TILES // 8 - 1))
                ahead, behind = T.plus(2), T.plus(-2)
                if ahead.exists:
                    node_stats(0, ahead)
                if behind.exists:
                    node_low(0, behind, 0)
                if ahead.exists:
                    node_mean(0, ahead)
                if behind.exists:
                    node_low(0, behind, 1)
                node_ext(0, T)
                if ahead.exists:
                    node_centre(0, ahead)

            dve.wait_ge(x_head, 16)
            sweep(dve, first_nodes, step=NODE_STEP)
            for k in range(TILES - 2, TILES):
                for s in range(2):
                    node_low(0, Tile(k), s)

            def build_mask(l, T):
                z_sign(l, T)
                mask_bits(l, T)
                if l == 0:
                    dve.wait_ge(S[0].centred, TILES)
                turn_bits(l, T)
                split_bits(l, T)

            for l in range(LAYERS):
                open_layer(l)
                build_mask(l, Tile(0))

                def tile(T):
                    done, ahead = T.plus(-1), T.plus(1)
                    nodes = done.exists and l == 0
                    if done.exists:
                        finish_tile(l, done)
                    if nodes:
                        node_stats(1, done)
                        node_mean(1, done)
                        node_centre(1, done)
                    if ahead.exists:
                        z_sign(l, ahead)
                        mask_bits(l, ahead)
                    if nodes:
                        node_ext(1, done)
                    if ahead.exists:
                        turn_bits(l, ahead)
                        split_bits(l, ahead)
                    if nodes:
                        for s in range(2):
                            node_low(1, done, s)

                sweep(dve, tile, trail=1)


_INS = ['x', 'adj', 'L0_gnn_W', 'L0_gnn_b_W', 'L0_gnn_a_vec', 'L0_gnn_b_a', 'L1_gnn_W_w', 'L1_gnn_W_b', 'L1_gnn_a']


def kernel(**inputs):
    import numpy as _np
    import concourse.bacc as _bacc
    from concourse import mybir as _mybir
    from concourse.bass_utils import run_bass_kernel_spmd as _run

    nc = _bacc.Bacc("TRN2", target_bir_lowering=False, num_devices=1)
    arrays, args = {}, []
    for name in _INS:
        a = _np.ascontiguousarray(inputs[name])
        arrays[f"in_{name}_dram"] = a
        args.append(nc.dram_tensor(f"in_{name}_dram", a.shape, _mybir.dt.from_np(a.dtype), kind="ExternalInput").ap())
    args.append(nc.dram_tensor("out_0_dram", (NODES, DIM), _mybir.dt.float32, kind="ExternalOutput").ap())
    gat_kernel(nc, *args)
    r = _run(nc, [arrays], core_ids=[0])
    return r.results[0]["out_0_dram"]
```

```python
import concourse.bass as bass
from concourse import mybir
from contextlib import ExitStack
import math

NODES = 8192
DIM = 128
LAYERS = 2
EPS = 1e-5
TILE = 128
TILES = NODES // TILE
QUADS = 4
QROWS = 32
SPAN = NODES // QUADS
RGROUPS = TILE // QROWS
BYTES = 4
BLOCKS = SPAN // (QROWS * BYTES)
CHUNKS = BLOCKS * BYTES
ONE = DIM
NEG_S, POS_T, LOG_B, LOG_D = DIM + 1, DIM + 2, DIM + 3, DIM + 4
EXT = DIM + 5
PART = DIM + 1
ROW = 2 * PART
KAPPA = 4.0
LEAK = 0.2
NO_EDGE = 9e15
MAX_T, MAX_S, MAX_W, MAX_B, MIN_W = 4.0, 32.0, 1.0, 128.0, 2.0 ** -6
LIMITS = [MAX_W, MAX_B, MAX_S, MAX_T]
EDGE_WORD = 0x20202020
LOW_Z_WORD = [0x10101010, 0x02020202]
SHIFT_G1 = [0, 3]
SHIFT_G2 = [1, 4]
KEEP_WORD = [0x30303030, 0x06060606]
VGROUPS = 4
PER_GROUP = BLOCKS // VGROUPS
X_GROUP = 16
X_HEAD = 8
HEAD = 4
NODE_STEP = 4


class Tile:

    def __init__(self, k, u=None, step=2):
        self.k, self.u, self.step = k, u, step
        self.p, self.p4 = k % 2, k % 4
        self.t = k if u is None else step * u + k
        self.n = k // 2 if u is None else step // 2 * u + k // 2
        self.n4 = k // 4 if u is None else u + k // 4

    def plus(self, d):
        return Tile(self.k + d, self.u, self.step)

    @property
    def exists(self):
        return self.u is not None or 0 <= self.k < TILES

    def wait_before(self, eng, sem, back):
        if self.u is not None or self.k - back >= 0:
            eng.wait_ge(sem, self.t - back + 1)


def sweep(eng, body, trail=0, step=2, head=HEAD):
    end = TILES - step
    for k in range(head):
        body(Tile(k))
    with eng.Fori(head // step, end // step) as u:
        for k in range(step):
            body(Tile(k, u, step))
    for k in range(end, TILES + trail):
        body(Tile(k))


def gat_kernel(nc, x, adj, w_0, b_w_0, a_vec_0, b_a_0, w_1, b_w_1, a_1, out):
    F32, F16, I8, I32, U32, FP8 = (mybir.dt.float32, mybir.dt.float16, mybir.dt.int8, mybir.dt.int32,
                                   mybir.dt.uint32, mybir.dt.float8e4)
    ALU, ACT, AX = mybir.AluOpType, mybir.ActivationFunctionType, mybir.AxisListType
    ds = bass.ds

    mask_dram = nc.dram_tensor("mask_bytes", (TILES // 2, 128, NODES), I8, kind="Internal").ap()
    rows_dram = [nc.dram_tensor(f"node_rows_{l}", (TILES, TILE, 2 * ROW), F16, kind="Internal").ap() for l in range(LAYERS)]
    st_dram = [nc.dram_tensor(f"neg_s_and_t_{l}", (2, NODES), F32, kind="Internal").ap() for l in range(LAYERS)]
    x1_dram = nc.dram_tensor("x_after_layer_0", (NODES, DIM), F32, kind="Internal").ap()

    with ExitStack() as ctx:
        def sb(name, shape, dt):
            return ctx.enter_context(nc.sbuf_tensor(name, shape, dt))

        def ps(name):
            return ctx.enter_context(nc.psum_tensor(name, [128, 512], F32))

        def sem(name):
            return ctx.enter_context(nc.semaphore(name))

        adj_sb = sb("adj_sb", [128, RGROUPS, SPAN], I32)
        sign_a = sb("sign_a", [128, 2, NODES], I8)
        sign_z = sb("sign_z", [128, 2, NODES], I8)
        pair_a = sb("pair_a", [128, NODES], I8)
        masks = sb("masks", [128, 2, 2, NODES], I8)
        g1, g2 = masks[:, 0, :, :], masks[:, 1, :, :]
        x_all = masks[:].rearrange("p m s c -> p (m s c)").bitcast(F32).rearrange("p (t d) -> p t d", d=DIM)
        picks = sign_z[:].rearrange("p s c -> p (s c)").bitcast(F32)
        pick_s = picks[:, 0:RGROUPS * 128].rearrange("p (r q) -> p r q", q=128)
        pick_t = picks[:, RGROUPS * 128:(RGROUPS + BLOCKS) * 128].rearrange("p (b q) -> p b q", q=128)
        t_row = sb("t_row", [128, SPAN], F32)
        node_rows = sb("node_rows", [128, CHUNKS, 2 * ROW], F16)
        nat = sb("nat", [128, 2 * TILES], F32)
        nat_t = sb("nat_t", [128, TILE], F32)
        neg_s = sb("neg_s", [128, TILES * RGROUPS], F32)
        coef_a = sb("coef_a", [128, TILES], F32)
        coef_c = sb("coef_c", [128, TILES], F32)
        h_sum = sb("h_sum", [128, DIM], F32)
        h_mean = sb("h_mean", [128, DIM], F32)
        part_a = sb("part_a", [128, 2, ROW], F32)
        part_ac = sb("part_ac", [128, 2, ROW], F32)
        joined = sb("joined", [128, 2, PART], F32)
        empty = sb("empty", [128, 2, 1], F32)
        den = sb("den", [128, 2, 1], F32)
        rden = sb("rden", [128, 2, 1], F32)
        numer = sb("numer", [128, 2, DIM], F32)
        x_old = sb("x_old", [128, 2, DIM], F32)
        x_new = sb("x_new", [128, 2, DIM], F32)
        stats = sb("stats", [128, 2, 6], F32)
        mean_var = sb("mean_var", [128, 2, 2], F32)
        var_eps = sb("var_eps", [128, 2, 1], F32)
        rstd = sb("rstd", [128, 2, 1], F32)
        centred = sb("centred", [128, 2, DIM], F32)
        centred_t = sb("centred_t", [128, 2, DIM], F32)
        ext = sb("ext", [128, 2, EXT], F32)
        b_and_d = sb("b_and_d", [128, 2, 2], F32)
        row_parts = sb("row_parts", [128, 4, 2 * ROW], F16)
        ident = sb("ident", [128, 128], F32)
        averager = sb("averager", [128, 128], F32)
        minus_half = sb("minus_half", [128, 1], F32)
        w_raw = [sb(f"w_raw_{l}", [128, 128], F32) for l in range(LAYERS)]
        w_tr = [sb(f"w_tr_{l}", [128, 128], F32) for l in range(LAYERS)]
        a_raw = [sb(f"a_raw_{l}", [128, 2], F32) for l in range(LAYERS)]
        b_raw = [sb(f"b_raw_{l}", [128, 1], F32) for l in range(LAYERS)]
        b_a_sb = sb("b_a_sb", [128, 1], F32)
        b_wide = [sb(f"b_wide_{l}", [128, 128], F32) for l in range(LAYERS)]
        id_and_a = [sb(f"id_and_a_{l}", [128, EXT], F32) for l in range(LAYERS)]
        w_ext = [sb(f"w_ext_{l}", [128, EXT], F32) for l in range(LAYERS)]
        bias = [sb(f"bias_{l}", [128, EXT], F32) for l in range(LAYERS)]

        n_limits = len(LIMITS)
        largest = sb("largest", [128, LAYERS * n_limits], F32)
        limit_row = sb("limit_row", [128, LAYERS * n_limits], F32)
        broken = sb("broken", [128, LAYERS * (n_limits + 1)], F32)
        verdict = sb("verdict", [128, 2], F32)
        use_general = sb("use_general", [128, 1], I32)

        acc = [[ps(f"acc_{p}_{s}") for s in range(2)] for p in range(2)]
        ps_t = [ps(f"ps_t_{p}") for p in range(2)]
        t_banks = acc[0] + acc[1]
        ps_h = ps("ps_h")
        ps_mean = ps("ps_mean")

        weights_loaded, ident_ready, picks_ready = sem("weights_loaded"), sem("ident_ready"), sem("picks_ready")
        setup_pe, setup_dve = sem("setup_pe"), sem("setup_dve")
        x_head, x_rest, rows_free = sem("x_head"), sem("x_rest"), sem("rows_free")
        adj_loaded = [sem(f"adj_loaded_{r}") for r in range(RGROUPS)]
        cast_done = sem("cast_done")
        packed, pair_stored, pair_loaded = sem("packed"), sem("pair_stored"), sem("pair_loaded")

        class LayerSems:
            def __init__(self, l):
                self.zsign_act, self.zsign_dve = sem(f"zsign_act_{l}"), sem(f"zsign_dve_{l}")
                self.edge_bits, self.turned = sem(f"edge_bits_{l}"), sem(f"turned_{l}")
                self.g1_ready, self.g_ready = sem(f"g1_ready_{l}"), sem(f"g_ready_{l}")
                self.tile_summed = sem(f"tile_summed_{l}")
                self.part_a, self.part_ac, self.fin = sem(f"part_a_{l}"), sem(f"part_ac_{l}"), sem(f"fin_{l}")
                self.x_old = [sem(f"x_old_{l}_{p}") for p in range(2)]
                self.x_stored = [sem(f"x_stored_{l}_{p}") for p in range(2)]
                self.stats, self.mean_var = sem(f"stats_{l}"), sem(f"mean_var_{l}")
                self.centred, self.var_eps, self.rstd = sem(f"centred_{l}"), sem(f"var_eps_{l}"), sem(f"rstd_{l}")
                self.turned_ps, self.centred_t = sem(f"turned_ps_{l}"), sem(f"centred_t_{l}")
                self.h_raw, self.ext = sem(f"h_raw_{l}"), sem(f"ext_{l}")
                self.h_sum, self.h_mean, self.st_kept = sem(f"h_sum_{l}"), sem(f"h_mean_{l}"), sem(f"st_kept_{l}")
                self.b_and_d, self.high_b, self.high_d, self.low = \
                    sem(f"b_and_d_{l}"), sem(f"high_b_{l}"), sem(f"high_d_{l}"), sem(f"low_{l}")
                self.rows_stored = [sem(f"rows_stored_{l}_{p}") for p in range(4 - 2 * l)]
                self.nat_ps, self.nat_sb = sem(f"nat_ps_{l}"), sem(f"nat_sb_{l}")
                self.s_picked, self.t_picked = sem(f"s_picked_{l}"), sem(f"t_picked_{l}")
                self.t_row_dve, self.t_row_act = sem(f"t_row_dve_{l}"), sem(f"t_row_act_{l}")
                self.neg_s, self.mean_kept, self.coefs = sem(f"neg_s_{l}"), sem(f"mean_kept_{l}"), sem(f"coefs_{l}")
                self.rows_loaded = [sem(f"rows_loaded_{l}_{g}") for g in range(VGROUPS)]

        S = [LayerSems(l) for l in range(LAYERS)]
        broken_known, broken_counted, path_known = sem("broken_known"), sem("broken_counted"), sem("path_known")
        limits = sem("limits")
        x_src = [x, x1_dram]
        x_dst = [x1_dram, out]

        def row_slot(l, T):
            return (T.p4, T.n4) if l == 0 else (T.p, T.n)

        FIN = 6

        def x_of(l, T):
            return x_all[:, ds(T.t, 1), :].rearrange("p o d -> p (o d)") if l == 0 else x_new[:, T.p, :]

        fast_path = ctx.enter_context(ExitStack())
        block = fast_path.enter_context(nc.Block())

        @block.sync
        def _(sp):
            def load_adj(T, r):
                for a in range(QUADS):
                    sp.nop(nofuse=True)
                    sp.dma_start(adj_sb[QROWS * a:QROWS * (a + 1), r, :],
                                 adj[ds(T.t * TILE + QROWS * r, QROWS), SPAN * a:SPAN * (a + 1)]) \
                      .then_inc(adj_loaded[r], 16)

            def load_x_old(l, T):
                if T.u is not None or T.k >= 2:
                    sp.wait_ge(S[l].fin, FIN * (T.t - 1))
                sp.nop(nofuse=True)
                sp.dma_start(x_old[:, T.p, :], x_src[l][ds(T.t * TILE, TILE), :]).then_inc(S[l].x_old[T.p], 16)

            def store_x_new(l, T):
                sp.wait_ge(S[l].fin, FIN * (T.t + 1))
                sp.nop(nofuse=True)
                sp.dma_start(x_dst[l][ds(T.t * TILE, TILE), :], x_new[:, T.p, :]).then_inc(S[l].x_stored[T.p], 16)

            def store_rows(l, T):
                sp.wait_ge(S[l].low, T.t + 1)
                sp.nop(nofuse=True)
                slot, _ = row_slot(l, T)
                sp.dma_start(rows_dram[l][ds(T.t, 1), :, :].rearrange("o p r -> p (o r)"), row_parts[:, slot, :]) \
                  .then_inc(S[l].rows_stored[slot], 16)

            def load_rows(l, a, g):
                src = rows_dram[l][BLOCKS * a + PER_GROUP * g:BLOCKS * a + PER_GROUP * (g + 1), :, :]
                dst = node_rows[QROWS * a:QROWS * (a + 1), BYTES * PER_GROUP * g:BYTES * PER_GROUP * (g + 1), :]
                sp.dma_start(dst.rearrange("p (b k) r -> p b (k r)", k=BYTES),
                             src.rearrange("b (j k) r -> j b (k r)", k=BYTES)).then_inc(S[l].rows_loaded[g], 16)

            sp.dma_start(w_raw[0][:], w_0).then_inc(weights_loaded, 16)
            sp.dma_start(w_raw[1][:], w_1).then_inc(weights_loaded, 16)
            x_tiles = x.rearrange("(t m) d -> m t d", m=TILE)
            sp.dma_start(x_all[:, 0:X_GROUP, :], x_tiles[:, 0:X_GROUP, :]).then_inc(x_head, 16)
            with nc.allow_non_contiguous_dma(reason="weight vectors onto partitions, once"):
                sp.dma_start(a_raw[0][:], a_vec_0.rearrange("(c p) -> p c", p=DIM)).then_inc(weights_loaded, 16)
                sp.dma_start(a_raw[1][:], a_1.rearrange("(c p) o -> p (c o)", p=DIM)).then_inc(weights_loaded, 16)
                sp.dma_start(b_raw[0][:], b_w_0.rearrange("(p o) -> p o", o=1)).then_inc(weights_loaded, 16)
                sp.dma_start(b_raw[1][:], b_w_1.rearrange("(p o) -> p o", o=1)).then_inc(weights_loaded, 16)
                sp.dma_start(b_a_sb[:], b_a_0.partition_broadcast(128)).then_inc(weights_loaded, 16)

            def load_x_group(g):
                group = slice(X_GROUP * g, X_GROUP * (g + 1))
                sp.dma_start(x_all[:, group, :], x_tiles[:, group, :]).then_inc(x_rest, 16)

            load_x_group(1)
            def load_quadrant(a):
                for p in range(4):
                    sp.wait_ge(S[0].rows_stored[p], 16 * BLOCKS // 4 * (a + 1))
                for g in range(VGROUPS):
                    load_rows(0, a, g)

            adj_after = [BLOCKS, 2 * BLOCKS, 2 * BLOCKS + 3, 3 * BLOCKS]
            for a in range(QUADS):
                for k in range(BLOCKS * a, BLOCKS * a + NODE_STEP):
                    store_rows(0, Tile(k))
                    if k in (0, 2):
                        load_x_group(2 + k // 2)
                    if k in adj_after:
                        load_adj(Tile(0), adj_after.index(k))
                if a:
                    load_quadrant(a - 1)
                with sp.Fori(BLOCKS // NODE_STEP * a + 1, BLOCKS // NODE_STEP * (a + 1)) as u:
                    for k in range(NODE_STEP):
                        store_rows(0, Tile(k, u, NODE_STEP))
            load_quadrant(QUADS - 1)

            load_x_old(0, Tile(0))
            load_x_old(0, Tile(1))

            def store_pair(T):
                sp.wait_ge(packed, T.t + 1)
                sp.nop(nofuse=True)
                sp.dma_start(mask_dram[ds(T.n, 1), :, :].rearrange("o p c -> p (o c)"), pair_a[:]).then_inc(pair_stored, 16)

            def load_pair(T):
                T.wait_before(sp, S[1].edge_bits, 1)
                sp.nop(nofuse=True)
                sp.dma_start(pair_a[:], mask_dram[ds(T.n, 1), :, :].rearrange("o p c -> p (o c)")).then_inc(pair_loaded, 16)

            def layer_0_tile(T):
                if T.plus(1).exists:
                    for r in range(RGROUPS):
                        sp.wait_ge(cast_done, RGROUPS * T.t + r + 1)
                        load_adj(T.plus(1), r)
                if T.p == 0 and T.plus(-1).exists:
                    store_pair(T.plus(-1))
                if T.plus(-3).exists:
                    store_x_new(0, T.plus(-3))
                    load_x_old(0, T.plus(-1))
                if T.plus(-4).exists:
                    store_rows(1, T.plus(-4))

            sweep(sp, layer_0_tile)
            load_x_old(0, Tile(TILES - 1))

            def reload_rows(g):
                for a in range(QUADS):
                    if (a, g) != (QUADS - 1, VGROUPS - 1):
                        load_rows(1, a, g)

            store_rows(1, Tile(TILES - 4))
            store_x_new(0, Tile(TILES - 3))
            for p in range(2):
                sp.wait_ge(S[1].rows_stored[p], 16 * (TILES // 2 - PER_GROUP // 2))
            sp.wait_ge(rows_free, 1)
            reload_rows(0)
            store_rows(1, Tile(TILES - 3))
            store_x_new(0, Tile(TILES - 2))
            store_pair(Tile(TILES - 1))
            sp.wait_ge(pair_stored, 16 * TILES // 2)
            load_pair(Tile(0))
            for g in range(1, VGROUPS - 1):
                sp.wait_ge(rows_free, g + 1)
                reload_rows(g)
            sp.wait_ge(S[0].tile_summed, TILES)
            reload_rows(VGROUPS - 1)
            store_x_new(0, Tile(TILES - 1))
            store_rows(1, Tile(TILES - 2))
            store_rows(1, Tile(TILES - 1))

            for p in range(2):
                sp.wait_ge(S[1].rows_stored[p], 16 * TILES // 2)
            load_rows(1, QUADS - 1, VGROUPS - 1)
            for p in range(2):
                sp.wait_ge(S[0].x_stored[p], 16 * TILES // 2)
            load_x_old(1, Tile(0))
            load_x_old(1, Tile(1))

            def layer_1_tile(T):
                if T.p == 1 and T.plus(1).exists:
                    load_pair(T.plus(1))
                if T.plus(-2).exists:
                    store_x_new(1, T.plus(-2))
                    load_x_old(1, T)

            sweep(sp, layer_1_tile)
            store_x_new(1, Tile(TILES - 2))
            store_x_new(1, Tile(TILES - 1))
            for p in range(2):
                sp.wait_ge(S[1].x_stored[p], 16 * TILES // 2)

        @block.gpsimd
        def _(pool):
            pool.memset(minus_half[:], -0.5).then_inc(ident_ready, 1)
            pool.memset(averager[:], 1.0 / NODES).then_inc(ident_ready, 1)
            pool.memset(ident[:], 0.0).then_inc(ident_ready, 1)
            pool.wait_ge(ident_ready, 3)
            pool.affine_select(out=ident[:], in_=ident[:], compare_op=ALU.not_equal, fill=1.0, base=0,
                               pattern=[[-1, 128]], channel_multiplier=1).then_inc(ident_ready, 1)
            pool.wait_ge(ident_ready, 4)
            t_columns = ident[:, TILES:2 * TILES].rearrange("p (a b) -> p b a", a=QUADS)

            def build_picks():
                for r in range(RGROUPS):
                    pool.tensor_copy(pick_s[:, r, :].rearrange("p (a i) -> p a i", a=QUADS),
                                     ident[:, QROWS * r:QROWS * (r + 1)].unsqueeze(1).to_broadcast([128, QUADS, QROWS])) \
                        .then_inc(picks_ready, 1)
                for b in range(BLOCKS):
                    pool.tensor_copy(pick_t[:, b, :].rearrange("p (a i) -> p a i", a=QUADS),
                                     t_columns[:, b, :].unsqueeze(2).to_broadcast([128, QUADS, QROWS])).then_inc(picks_ready, 1)

            build_picks()
            nat_v = nat[:].rearrange("p (c t) -> p c t", c=2)

            def node_step(l, T):
                pool.wait_ge(S[l].var_eps, T.t + 1)
                T.wait_before(pool, S[l].ext, 2)
                pool.nop(nofuse=True)
                pool.tensor_tensor(rstd[:, T.p, :], var_eps[:, T.p, :], minus_half[:], ALU.pow).then_inc(S[l].rstd, 1)

            def node_rest(l, T):
                pool.wait_ge(S[l].ext, T.t + 1)
                if T.u is None and T.k == 0:
                    if l:
                        pool.wait_ge(S[0].h_mean, 1)
                    pool.tensor_copy(h_sum[:], ext[:, T.p, 0:DIM]).then_inc(S[l].h_sum, 1)
                else:
                    pool.wait_ge(S[l].h_sum, T.t)
                    pool.nop(nofuse=True)
                    pool.tensor_tensor(h_sum[:], h_sum[:], ext[:, T.p, 0:DIM], ALU.add).then_inc(S[l].h_sum, 1)
                pool.tensor_copy(nat_v[:, :, ds(T.t, 1)], ext[:, T.p, NEG_S:POS_T + 1].rearrange("p (c o) -> p c o", o=1)) \
                    .then_inc(S[l].st_kept, 1)
                if l == 0:
                    return
                pool.wait_ge(S[l].b_and_d, T.t + 1)
                slot, used = row_slot(l, T)
                if T.u is not None or used:
                    pool.wait_ge(S[l].rows_stored[slot], 16 * used)
                pool.nop(nofuse=True)
                pool.tensor_scalar(row_parts[:, slot, ROW:ROW + PART], ext[:, T.p, 0:PART], b_and_d[:, T.p, 1:2], 1.0,
                                   ALU.mult, ALU.mult).then_inc(S[l].high_d, 1)

            for l in range(LAYERS):
                if l:
                    pool.wait_ge(S[0].nat_ps, 1)
                    pool.wait_ge(S[0].coefs, 2)
                    pool.wait_ge(limits, n_limits)

                def body(T):
                    if l and T.u is None and T.k == TILES - 2:
                        pool.wait_ge(S[0].turned, TILES)
                        build_picks()
                    if T.exists:
                        node_step(l, T)
                    rest = T.plus(l - 1)
                    if rest.exists:
                        node_rest(l, rest)

                sweep(pool, body, trail=1 - l, step=[NODE_STEP, 2][l])

        @block.tensor
        def _(pe):
            pe.wait_ge(weights_loaded, 7 * 16)
            pe.wait_ge(ident_ready, 4)
            for l in range(LAYERS):
                pe.transpose(ps_t[l][:, 0:128], w_raw[l][:], ident[:]).then_inc(setup_pe, 1)
            pe.wait_ge(setup_dve, LAYERS)
            w_oi = [w_raw[0], w_tr[1]]
            for l in range(LAYERS):
                pe.matmul(ps_h[:, 8 * l:8 * l + 5], w_oi[l][:], id_and_a[l][:, DIM:EXT], start=True, stop=True) \
                  .then_inc(setup_pe, 1)
                pe.matmul(acc[0][l][:, 0:EXT], b_wide[l][:], id_and_a[l][:], start=True, stop=True).then_inc(setup_pe, 1)
            pe.wait_ge(setup_dve, LAYERS + 1)

            def turn(l, T):
                pe.wait_ge(S[l].centred, T.t + 1)
                T.wait_before(pe, S[l].centred_t, 2)
                pe.transpose(ps_t[T.p][:, 0:DIM], centred[:, T.p, :], ident[:]).then_inc(S[l].turned_ps, 1)

            def project(l, T):
                pe.wait_ge(S[l].centred_t, T.t + 1)
                T.wait_before(pe, S[l].ext, 1)
                pe.matmul(ps_h[:, 0:EXT], centred_t[:, T.p, :], w_ext[l][:], start=True, stop=True).then_inc(S[l].h_raw, 1)

            def close_nodes(l):
                pe.wait_ge(S[l].st_kept, TILES)
                pe.wait_ge(S[l].centred_t, TILES)
                pe.transpose(ps_t[0][:, 0:128], nat[:], ident[:]).then_inc(S[l].nat_ps, 1)
                pe.wait_ge(picks_ready, (l + 1) * (RGROUPS + BLOCKS))
                for r in range(RGROUPS):
                    pe.matmul(ps_t[1][:, TILES * r:TILES * (r + 1)], pick_s[:, r, :], nat[:, 0:TILES], start=True, stop=True) \
                      .then_inc(S[l].s_picked, 1)
                if l:
                    pe.wait_ge(S[l - 1].part_a, TILES)
                    pe.wait_ge(S[l - 1].part_ac, TILES)
                pe.wait_ge(S[l].nat_sb, 1)
                for b in range(BLOCKS):
                    pe.matmul(t_banks[b // 4][:, 128 * (b % 4):128 * (b % 4 + 1)], pick_t[:, b, :], nat_t[:],
                              start=True, stop=True).then_inc(S[l].t_picked, 1)
                pe.wait_ge(S[l].h_sum, TILES)
                pe.matmul(ps_mean[:, 0:DIM], averager[:], h_sum[:], start=True, stop=True).then_inc(S[l].h_mean, 1)

            def first_nodes(T):
                if T.u is None and T.k == 0:
                    turn(0, T)
                    turn(0, T.plus(1))
                project(0, T)
                if T.plus(2).exists:
                    turn(0, T.plus(2))

            sweep(pe, first_nodes, step=NODE_STEP)
            close_nodes(0)

            turn_at, project_at = 8, 24

            for l in range(LAYERS):
                def tile(T):
                    pe.wait_ge(S[l].g_ready, T.t + 1)
                    T.wait_before(pe, S[l].part_a, 2)
                    T.wait_before(pe, S[l].part_ac, 2)
                    pe.nop(nofuse=True)
                    stationary = [m[:, T.p, :].bitcast(FP8).rearrange("p (b i k) -> p b k i", b=BLOCKS, k=BYTES)
                                  for m in (g1, g2)]
                    for c in range(CHUNKS):
                        if T.u is None and T.k == 0 and c % (CHUNKS // VGROUPS) == 0:
                            pe.wait_ge(S[l].rows_loaded[c // (CHUNKS // VGROUPS)], 16 * QUADS)
                        for s in range(2):
                            mm = pe.matmul(acc[T.p][s][:, 0:ROW], stationary[s][:, c // BYTES, c % BYTES, :],
                                           node_rows[:, c, ROW * s:ROW * (s + 1)],
                                           start=(c == 0), stop=(c == CHUNKS - 1), skip_group_check=True)
                        if l == 0 and T.u is None and T.k == TILES - 1 and c % (CHUNKS // VGROUPS) == CHUNKS // VGROUPS - 1 \
                                and c < CHUNKS - 1:
                            mm.then_inc(rows_free, 1)
                        if l == 0 and T.plus(-2).exists:
                            if c == turn_at:
                                turn(1, T.plus(-2))
                            if c == project_at:
                                project(1, T.plus(-2))
                    mm.then_inc(S[l].tile_summed, 1)

                if l == 1:
                    pe.wait_ge(broken_known, 1)
                    pe.wait_ge(S[1].mean_kept, 1)
                    pe.matmul(ps_mean[:, DIM:DIM + LAYERS * (n_limits + 1)], averager[:], broken[:], start=True, stop=True) \
                      .then_inc(broken_counted, 1)
                if l == 0:
                    pe.wait_ge(S[0].mean_kept, 1)
                    pe.wait_ge(S[0].nat_sb, 1)
                    pe.wait_ge(S[0].neg_s, 1)
                pe.wait_ge(S[l].t_row_dve, 2)
                pe.wait_ge(S[l].t_row_act, 2)
                sweep(pe, tile)
                if l == 0:
                    for k in range(TILES - 2, TILES):
                        turn(1, Tile(k))
                        project(1, Tile(k))
                    close_nodes(1)

        @block.scalar
        def _(act):
            def node_copy(l, T):
                act.wait_ge(S[l].turned_ps, T.t + 1)
                T.wait_before(act, S[l].h_raw, 2)
                nc.scalar.copy(centred_t[:, T.p, :], ps_t[T.p][:, 0:DIM]).then_inc(S[l].centred_t, 1)

            def node_high(l, T):
                act.wait_ge(S[l].ext, T.t + 1)
                T.wait_before(act, S[l].high_b, 2)
                T.wait_before(act, S[l].high_d, 2)
                T.wait_before(act, S[l].low, 2)
                slot, used = row_slot(l, T)
                if T.u is not None or used:
                    act.wait_ge(S[l].rows_stored[slot], 16 * used)
                nc.scalar.activation(b_and_d[:, T.p, :], ext[:, T.p, LOG_B:LOG_D + 1], ACT.Exp).then_inc(S[l].b_and_d, 1)
                act.wait_ge(S[l].b_and_d, T.t + 1)
                nc.scalar.activation(row_parts[:, slot, 0:PART], ext[:, T.p, 0:PART], ACT.Copy, scale=b_and_d[:, T.p, 0:1]) \
                  .then_inc(S[l].high_b, 1)
                if l == 0:
                    nc.scalar.activation(row_parts[:, slot, ROW:ROW + PART], ext[:, T.p, 0:PART], ACT.Copy,
                                         scale=b_and_d[:, T.p, 1:2]).then_inc(S[l].high_d, 1)

            def cast(T, r):
                if r == 0 and (T.u is not None or T.k >= 2):
                    act.wait_ge(S[0].edge_bits, T.t - 1)
                    act.wait_ge(packed, T.t - 1)
                act.wait_ge(adj_loaded[r], 16 * QUADS * (T.t + 1))
                nc.scalar.activation(sign_a[:, T.p, SPAN * r:SPAN * (r + 1)], adj_sb[:, r, :], ACT.Sign, scale=-1.0) \
                  .then_inc(cast_done, 1)

            def z_sign(l, T, r):
                if r == 0:
                    T.wait_before(act, S[l].turned, 2)
                nc.scalar.activation(sign_z[:, T.p, SPAN * r:SPAN * (r + 1)], t_row[:], ACT.Sign, scale=-1.0,
                                     bias=neg_s[:, ds(RGROUPS * T.t + r, 1)]).then_inc(S[l].zsign_act, 1)

            def part_one(l, T):
                act.wait_ge(S[l].tile_summed, T.t + 1)
                T.wait_before(act, S[l].part_ac, 2)
                nc.scalar.activation(part_a[:, T.p, :], acc[T.p][0][:, 0:ROW], ACT.Copy, scale=coef_a[:, ds(T.t, 1)]) \
                  .then_inc(S[l].part_a, 1)

            def keep_t(l):
                if l:
                    act.wait_ge(S[l - 1].zsign_act, 2 * TILES)
                    act.wait_ge(S[l - 1].zsign_dve, 2 * TILES)
                for j in range(2, 4):
                    act.wait_ge(S[l].t_picked, 4 * (j + 1))
                    nc.scalar.copy(t_row[:, 512 * j:512 * (j + 1)], t_banks[j][:]).then_inc(S[l].t_row_act, 1)
                act.wait_ge(S[l].t_row_act, 2)
                act.wait_ge(S[l].t_row_dve, 2)

            def open_layer(l):
                act.wait_ge(S[l].st_kept, TILES)
                if l:
                    act.wait_ge(S[l - 1].part_ac, TILES)
                    act.wait_ge(S[l - 1].part_a, TILES)
                nc.scalar.activation(coef_a[:], nat[:, 0:TILES], ACT.Exp, scale=-1.0).then_inc(S[l].coefs, 1)
                nc.scalar.activation(coef_c[:], nat[:, 0:TILES], ACT.Exp, scale=-LEAK).then_inc(S[l].coefs, 1)

            def first_nodes(T):
                if T.u is None and T.k == 0:
                    node_copy(0, T)
                if T.plus(1).exists:
                    node_copy(0, T.plus(1))
                node_high(0, T)
                if T.u is None and T.k >= TILES - RGROUPS:
                    cast(Tile(0), T.k - (TILES - RGROUPS))

            sweep(act, first_nodes, step=NODE_STEP)
            open_layer(0)
            keep_t(0)
            act.wait_ge(S[0].neg_s, 1)
            act.wait_ge(S[0].coefs, 2)
            for r in range(2):
                z_sign(0, Tile(0), r)
            for r in range(RGROUPS):
                cast(Tile(1), r)
            for r in range(2):
                z_sign(0, Tile(1), r)

            def layer_0_tile(T):
                before, done, ahead = T.plus(-2), T.plus(-1), T.plus(2)
                if done.exists:
                    part_one(0, done)
                if ahead.exists:
                    cast(ahead, 0)
                if before.exists:
                    node_copy(1, before)
                if ahead.exists:
                    z_sign(0, ahead, 0)
                    cast(ahead, 1)
                    z_sign(0, ahead, 1)
                    cast(ahead, 2)
                if before.exists:
                    node_high(1, before)
                if ahead.exists:
                    cast(ahead, 3)

            sweep(act, layer_0_tile, trail=2)
            open_layer(1)
            keep_t(1)
            act.wait_ge(S[1].neg_s, 1)
            act.wait_ge(S[1].coefs, 2)
            act.wait_ge(S[0].turned, TILES)
            for k in range(2):
                for r in range(2):
                    z_sign(1, Tile(k), r)

            def layer_1_tile(T):
                if T.plus(-1).exists:
                    part_one(1, T.plus(-1))
                if T.plus(2).exists:
                    for r in range(2):
                        z_sign(1, T.plus(2), r)

            sweep(act, layer_1_tile, trail=1)

        @block.vector
        def _(dve):
            def node_stats(l, T):
                if l:
                    dve.wait_ge(S[0].fin, FIN * (T.t + 1))
                T.wait_before(dve, S[l].mean_var, 2)
                nc.vector.bn_stats(stats[:, T.p, :], x_of(l, T)).then_inc(S[l].stats, 1)

            def node_mean(l, T):
                dve.wait_ge(S[l].stats, T.t + 1)
                T.wait_before(dve, S[l].centred, 2)
                T.wait_before(dve, S[l].var_eps, 2)
                dve.nop(nofuse=True)
                nc.vector.bn_aggr(mean_var[:, T.p, :], stats[:, T.p, :]).then_inc(S[l].mean_var, 1)

            def node_centre(l, T):
                dve.wait_ge(S[l].mean_var, T.t + 1)
                T.wait_before(dve, S[l].turned_ps, 2)
                nc.vector.tensor_scalar(centred[:, T.p, :], x_of(l, T), mean_var[:, T.p, 0:1], 0.0, ALU.subtract, ALU.max) \
                    .then_inc(S[l].centred, 1)
                T.wait_before(dve, S[l].rstd, 2)
                nc.vector.tensor_scalar(var_eps[:, T.p, :], mean_var[:, T.p, 1:2], EPS, None, ALU.add) \
                    .then_inc(S[l].var_eps, 1)

            dve.wait_ge(x_head, 16)
            for k in range(2):
                node_stats(0, Tile(k))
            for k in range(2):
                node_mean(0, Tile(k))
            for k in range(2):
                node_centre(0, Tile(k))

            dve.wait_ge(weights_loaded, 7 * 16)
            dve.wait_ge(ident_ready, 4)
            steps = sem("setup_steps")
            n_steps = [0]

            def step(ins):
                n_steps[0] += 1
                ins.then_inc(steps, 1)

            def settle():
                dve.wait_ge(steps, n_steps[0])

            for l in range(LAYERS):
                ia = id_and_a[l]
                step(nc.vector.tensor_copy(ia[:, 0:DIM], ident[:]))
                step(nc.vector.memset(ia[:, ONE:ONE + 1], 0.0))
                step(nc.vector.tensor_scalar(ia[:, NEG_S:NEG_S + 1], a_raw[l][:, 0:1], -1.0, None, ALU.mult))
                step(nc.vector.tensor_copy(ia[:, POS_T:POS_T + 1], a_raw[l][:, 1:2]))
                step(nc.vector.tensor_copy(ia[:, LOG_B:LOG_B + 1], a_raw[l][:, 1:2]))
                step(nc.vector.tensor_scalar(ia[:, LOG_D:LOG_D + 1], a_raw[l][:, 1:2], LEAK, None, ALU.mult))
                step(nc.vector.tensor_scalar(b_wide[l][:], ident[:], 0.0, b_raw[l][:, 0:1], ALU.mult, ALU.add))
            settle()
            for l in range(LAYERS):
                dve.wait_ge(setup_pe, l + 1)
                nc.vector.tensor_copy(w_tr[l][:], ps_t[l][:, 0:128]).then_inc(setup_dve, 1)
            dve.wait_ge(setup_dve, LAYERS)
            step(nc.vector.tensor_copy(w_ext[0][:, 0:DIM], w_tr[0][:]))
            step(nc.vector.tensor_copy(w_ext[1][:, 0:DIM], w_raw[1][:]))
            dve.wait_ge(setup_pe, 3 * LAYERS)
            for l in range(LAYERS):
                step(nc.vector.tensor_copy(w_ext[l][:, DIM:EXT], ps_h[:, 8 * l:8 * l + 5]))
                step(nc.vector.tensor_copy(bias[l][:], acc[0][l][:, 0:EXT]))
            settle()
            for l in range(LAYERS):
                step(nc.vector.tensor_scalar(bias[l][:, ONE:ONE + 1], bias[l][:, ONE:ONE + 1], 1.0, None, ALU.add))
                step(nc.vector.tensor_scalar(bias[l][:, LOG_B:EXT], bias[l][:, LOG_B:EXT], math.log(KAPPA), None, ALU.add))
            nc.vector.tensor_tensor(bias[0][:, NEG_S:NEG_S + 1], bias[0][:, NEG_S:NEG_S + 1], b_a_sb[:], ALU.subtract) \
                .then_inc(setup_dve, 1)
            settle()
            dve.wait_ge(setup_dve, LAYERS + 1)

            def node_ext(l, T):
                dve.wait_ge(S[l].h_raw, T.t + 1)
                dve.wait_ge(S[l].rstd, T.t + 1)
                T.wait_before(dve, S[l].high_b, 2)
                T.wait_before(dve, S[l].high_d, 2)
                T.wait_before(dve, S[l].h_sum, 2)
                T.wait_before(dve, S[l].st_kept, 2)
                T.wait_before(dve, S[l].low, 2)
                nc.vector.scalar_tensor_tensor(out=ext[:, T.p, :], in0=ps_h[:, 0:EXT], scalar=rstd[:, T.p, 0:1],
                                               in1=bias[l][:], op0=ALU.mult, op1=ALU.add).then_inc(S[l].ext, 1)

            def node_low(l, T, s):
                dve.wait_ge([S[l].high_b, S[l].high_d][s], T.t + 1)
                slot, _ = row_slot(l, T)
                ins = nc.vector.scalar_tensor_tensor(
                    out=row_parts[:, slot, ROW * s + PART:ROW * (s + 1)], in0=ext[:, T.p, 0:PART],
                    scalar=b_and_d[:, T.p, s:s + 1], in1=row_parts[:, slot, ROW * s:ROW * s + PART],
                    op0=ALU.mult, op1=ALU.subtract)
                if s == 1:
                    ins.then_inc(S[l].low, 1)

            def z_sign(l, T, r):
                if T.u is None and T.k < 2 and l:
                    dve.wait_ge(S[l - 1].turned, TILES)
                T.wait_before(dve, S[l].turned, 2)
                nc.vector.tensor_scalar(sign_z[:, T.p, SPAN * r:SPAN * (r + 1)], t_row[:],
                                        neg_s[:, ds(RGROUPS * T.t + r, 1)], -1.0, ALU.is_gt, ALU.mult) \
                  .then_inc(S[l].zsign_dve, 1)

            def mask_bits(l, T):
                if l == 0:
                    dve.wait_ge(cast_done, RGROUPS * (T.t + 1))
                    edges = sign_a[:, T.p, :].bitcast(U32)
                else:
                    dve.wait_ge(pair_loaded, 16 * (T.n + 1))
                    edges = pair_a[:].bitcast(U32)
                dve.wait_ge(S[l].zsign_act, 2 * (T.t + 1))
                dve.wait_ge(S[l].zsign_dve, 2 * (T.t + 1))
                bits = sign_z[:, T.p, :].bitcast(U32)
                nc.vector.scalar_tensor_tensor(out=bits, in0=bits, scalar=LOW_Z_WORD[T.p], in1=edges,
                                               op0=ALU.bitwise_xor, op1=ALU.bitwise_and).then_inc(S[l].edge_bits, 1)

            def pack(T):
                edges, pair = sign_a[:, T.p, :].bitcast(U32), pair_a[:].bitcast(U32)
                if T.p == 0:
                    if T.u is not None or T.k:
                        dve.wait_ge(pair_stored, 16 * T.n)
                    nc.vector.tensor_scalar(pair, edges, KEEP_WORD[0], None, ALU.bitwise_and).then_inc(packed, 1)
                else:
                    dve.wait_ge(packed, T.t)
                    nc.vector.scalar_tensor_tensor(out=pair, in0=edges, scalar=KEEP_WORD[1], in1=pair,
                                                   op0=ALU.bitwise_and, op1=ALU.bitwise_or).then_inc(packed, 1)

            def turn_bits(l, T):
                dve.wait_ge(S[l].edge_bits, T.t + 1)
                if T.u is None and T.k < 2 and l:
                    dve.wait_ge(S[l - 1].tile_summed, TILES)
                T.wait_before(dve, S[l].tile_summed, 2)
                nc.vector.transpose(g2[:, T.p, :].bitcast(U32).rearrange("p (b r i) -> p r b i", r=RGROUPS, i=QROWS),
                                    sign_z[:, T.p, :].bitcast(U32).rearrange("p (r b i) -> p r b i", r=RGROUPS, i=QROWS)) \
                  .then_inc(S[l].turned, 1)

            def split_g1(l, T):
                dve.wait_ge(S[l].turned, T.t + 1)
                words = g2[:, T.p, :].bitcast(U32)
                nc.vector.tensor_scalar(g1[:, T.p, :].bitcast(U32), words, SHIFT_G1[T.p], EDGE_WORD,
                                        ALU.logical_shift_left, ALU.bitwise_and).then_inc(S[l].g1_ready, 1)

            def split_g2(l, T):
                words = g2[:, T.p, :].bitcast(U32)
                dve.wait_ge(S[l].g1_ready, T.t + 1)
                nc.vector.tensor_scalar(words, words, SHIFT_G2[T.p], EDGE_WORD,
                                        ALU.logical_shift_left, ALU.bitwise_and).then_inc(S[l].g_ready, 1)

            def finish_weigh(l, T):
                dve.wait_ge(S[l].part_a, T.t + 1)
                dve.wait_ge(S[l].tile_summed, T.t + 1)
                nc.vector.scalar_tensor_tensor(out=part_ac[:, T.p, :], in0=acc[T.p][1][:, 0:ROW], scalar=coef_c[:, ds(T.t, 1)],
                                               in1=part_a[:, T.p, :], op0=ALU.mult, op1=ALU.add).then_inc(S[l].part_ac, 1)

            def finish_join(l, T):
                dve.wait_ge(S[l].part_ac, T.t + 1)
                nc.vector.tensor_tensor(joined[:, T.p, :], part_ac[:, T.p, 0:PART], part_ac[:, T.p, PART:ROW], ALU.add) \
                    .then_inc(S[l].fin, 1)

            def finish_empty(l, T):
                dve.wait_ge(S[l].fin, FIN * T.t + 1)
                nc.vector.tensor_scalar(empty[:, T.p, :], joined[:, T.p, DIM:PART], 0.0, None, ALU.is_equal) \
                    .then_inc(S[l].fin, 1)

            def finish_mean(l, T):
                dve.wait_ge(S[l].fin, FIN * T.t + 2)
                nc.vector.tensor_tensor(den[:, T.p, :], joined[:, T.p, DIM:PART], empty[:, T.p, :], ALU.add) \
                    .then_inc(S[l].fin, 1)
                nc.vector.scalar_tensor_tensor(out=numer[:, T.p, :], in0=h_mean[:], scalar=empty[:, T.p, :],
                                               in1=joined[:, T.p, 0:DIM], op0=ALU.mult, op1=ALU.add).then_inc(S[l].fin, 1)

            def finish_divide(l, T):
                dve.wait_ge(S[l].fin, FIN * T.t + 3)
                nc.vector.reciprocal(rden[:, T.p, :], den[:, T.p, :]).then_inc(S[l].fin, 1)

            def finish_add(l, T):
                dve.wait_ge(S[l].fin, FIN * T.t + 5)
                dve.wait_ge(S[l].x_old[T.p], 16 * (T.n + 1))
                if T.u is not None or T.k >= 2:
                    dve.wait_ge(S[l].x_stored[T.p], 16 * T.n)
                elif l:
                    dve.wait_ge(S[0].x_stored[T.p], 16 * TILES // 2)
                if l == 0:
                    T.wait_before(dve, S[1].centred, 2)
                nc.vector.scalar_tensor_tensor(out=x_new[:, T.p, :], in0=numer[:, T.p, :], scalar=rden[:, T.p, :],
                                               in1=x_old[:, T.p, :], op0=ALU.mult, op1=ALU.add).then_inc(S[l].fin, 1)

            n_limit_steps = [0]

            def limit_step(ins):
                n_limit_steps[0] += 1
                ins.then_inc(limits, 1)
                dve.wait_ge(limits, n_limit_steps[0])

            def keep_largest(l, k, values):
                limit_step(nc.vector.tensor_reduce(largest[:, n_limits * l + k:n_limits * l + k + 1], values, AX.X, ALU.max,
                                                   apply_absolute_value=True))

            def measure_layer(l):
                keep_largest(l, 0, w_ext[l][:, 0:DIM])
                keep_largest(l, 1, bias[l][:, 0:DIM])
                keep_largest(l, 2, nat[:, 0:TILES])
                keep_largest(l, 3, nat[:, TILES:2 * TILES])

            def mark_broken():
                for l in range(LAYERS):
                    for k in range(n_limits):
                        limit_step(nc.vector.memset(limit_row[:, n_limits * l + k:n_limits * l + k + 1], LIMITS[k]))
                    limit_step(nc.vector.tensor_scalar(broken[:, LAYERS * n_limits + l:LAYERS * n_limits + l + 1],
                                                       largest[:, n_limits * l:n_limits * l + 1], MIN_W, None, ALU.is_lt))
                nc.vector.tensor_tensor(broken[:, 0:LAYERS * n_limits], largest[:], limit_row[:], ALU.is_gt) \
                    .then_inc(broken_known, 1)

            def choose_path():
                dve.wait_ge(broken_counted, 1)
                counts = ps_mean[:, DIM:DIM + LAYERS * (n_limits + 1)]
                limit_step(nc.vector.tensor_reduce(verdict[:, 0:1], counts[:, 0:LAYERS * n_limits], AX.X, ALU.max))
                limit_step(nc.vector.tensor_reduce(verdict[:, 1:2], counts[:, LAYERS * n_limits:], AX.X, ALU.max))
                limit_step(nc.vector.tensor_scalar(verdict[:, 0:1], verdict[:, 0:1], 0.0, None, ALU.is_gt))
                limit_step(nc.vector.tensor_scalar(verdict[:, 1:2], verdict[:, 1:2], 128.0 / NODES, None, ALU.is_ge))
                nc.vector.tensor_tensor(use_general[:], verdict[:, 0:1], verdict[:, 1:2], ALU.max).then_inc(path_known, 1)

            def open_layer(l):
                dve.wait_ge(S[l].nat_ps, 1)
                if l:
                    dve.wait_ge(S[l - 1].t_picked, BLOCKS)
                    dve.wait_ge(S[l - 1].zsign_act, 2 * TILES)
                    dve.wait_ge(S[l - 1].zsign_dve, 2 * TILES)
                nc.vector.tensor_copy(nat_t[:], ps_t[0][:, 0:128]).then_inc(S[l].nat_sb, 1)
                dve.wait_ge(S[l].s_picked, RGROUPS)
                nc.vector.tensor_copy(neg_s[:].rearrange("p (t r) -> p r t", r=RGROUPS),
                                      ps_t[1][:, 0:RGROUPS * TILES].rearrange("p (r t) -> p r t", r=RGROUPS)) \
                    .then_inc(S[l].neg_s, 1)
                measure_layer(l)
                if l == LAYERS - 1:
                    mark_broken()
                for j in range(2):
                    dve.wait_ge(S[l].t_picked, 4 * (j + 1))
                    nc.vector.tensor_copy(t_row[:, 512 * j:512 * (j + 1)], t_banks[j][:]).then_inc(S[l].t_row_dve, 1)
                dve.wait_ge(S[l].h_mean, 1)
                nc.vector.tensor_copy(h_mean[:], ps_mean[:, 0:DIM]).then_inc(S[l].mean_kept, 1)
                dve.wait_ge(S[l].neg_s, 1)
                dve.wait_ge(S[l].t_row_dve, 2)
                dve.wait_ge(S[l].t_row_act, 2)
                dve.wait_ge(S[l].mean_kept, 1)
                dve.wait_ge(S[l].coefs, 2)

            def first_nodes(T):
                if T.u is None and T.k == X_HEAD - 1:
                    dve.wait_ge(x_rest, 16 * (TILES // X_GROUP - 1))
                ahead, behind = T.plus(2), T.plus(-2)
                if ahead.exists:
                    node_stats(0, ahead)
                if behind.exists:
                    node_low(0, behind, 0)
                if ahead.exists:
                    node_mean(0, ahead)
                if behind.exists:
                    node_low(0, behind, 1)
                if ahead.exists:
                    node_centre(0, ahead)
                node_ext(0, T)

            sweep(dve, first_nodes, step=NODE_STEP, head=X_HEAD)
            for k in range(TILES - 2, TILES):
                for s in range(2):
                    node_low(0, Tile(k), s)

            for l in range(LAYERS):
                open_layer(l)

                def tile(T):
                    ahead, done, before = T.plus(1), T.plus(-1), T.plus(-2)
                    done_nodes, before_nodes = l == 0 and done.exists, l == 0 and before.exists
                    if ahead.exists:
                        z_sign(l, ahead, 2)
                    if done.exists:
                        finish_weigh(l, done)
                    if ahead.exists:
                        z_sign(l, ahead, 3)
                    if done.exists:
                        finish_join(l, done)
                    if ahead.exists:
                        mask_bits(l, ahead)
                    if done.exists:
                        finish_empty(l, done)
                    if ahead.exists and l == 0:
                        pack(ahead)
                    if done.exists:
                        finish_mean(l, done)
                    if ahead.exists:
                        if l == 0 and T.u is None and T.k < 1:
                            dve.wait_ge(S[0].centred, TILES)
                        turn_bits(l, ahead)
                    if before_nodes:
                        node_ext(1, before)
                    if done.exists:
                        finish_divide(l, done)
                    if ahead.exists:
                        split_g1(l, ahead)
                    if done.exists:
                        finish_add(l, done)
                    if ahead.exists:
                        split_g2(l, ahead)
                    if done_nodes:
                        node_stats(1, done)
                    if before_nodes:
                        node_low(1, before, 0)
                    if done_nodes:
                        node_mean(1, done)
                    if before_nodes:
                        node_low(1, before, 1)
                    if done_nodes:
                        node_centre(1, done)

                tile(Tile(-1))
                if l == LAYERS - 1:
                    choose_path()
                sweep(dve, tile, trail=2 - l)

        fast_path.close()

        wide = node_rows[:].rearrange("p c r -> p (c r)").bitcast(F32)
        h_all = wide[:, 0:NODES].rearrange("p (t d) -> p t d", d=DIM)
        score = wide[:, NODES:2 * NODES]
        t_wide = masks[:].rearrange("p m s c -> p (m s c)").bitcast(F32)
        adj_rows = adj_sb[:].rearrange("p r c -> p (r c)")
        limit = adj_rows.bitcast(F32)
        row_max, row_sum, row_scale = den[:, 0, :], empty[:, 0, :], rden[:, 0, :]
        scalar_of = nat[:, 0:TILES]

        class GeneralSems:
            def __init__(self, l):
                self.x_loaded, self.x_normal, self.scaled = sem(f"gx_loaded_{l}"), sem(f"gx_normal_{l}"), sem(f"gx_scaled_{l}")
                self.node_steps, self.turned, self.copied = sem(f"gnode_steps_{l}"), sem(f"gturned_{l}"), sem(f"gcopied_{l}")
                self.projected, self.node_done = sem(f"gprojected_{l}"), sem(f"gnode_done_{l}")
                self.nat_turned, self.nat_copied = sem(f"gnat_turned_{l}"), sem(f"gnat_copied_{l}")
                self.st_stored, self.t_loaded = sem(f"gst_stored_{l}"), sem(f"gt_loaded_{l}")
                self.rows_loaded, self.row_steps = sem(f"grows_loaded_{l}"), sem(f"grow_steps_{l}")
                self.shifted, self.exp_done = sem(f"gshifted_{l}"), sem(f"gexp_done_{l}")
                self.p_turned, self.p_copied, self.p_used = sem(f"gp_turned_{l}"), sem(f"gp_copied_{l}"), sem(f"gp_used_{l}")
                self.x_done, self.x_stored = sem(f"gx_done_{l}"), sem(f"gx_stored_{l}")

        G = [GeneralSems(l) for l in range(LAYERS)]
        general_block = ctx.enter_context(nc.Block())

        def in_order(eng, counter, base, steps):
            done = [0]

            def step(ins):
                done[0] += 1
                assert done[0] <= steps
                ins.then_inc(counter, 1)
                eng.wait_ge(counter, base + done[0])
                eng.nop(nofuse=True)
            return step

        @general_block.sync
        def _(sp):
            with sp.If(sp.value_load(use_general[0:1, 0:1]) > 0):
                for l in range(LAYERS):
                    g = G[l]
                    with sp.Fori(0, TILES) as t:
                        sp.dma_start(x_old[:, 0, :], x_src[l][ds(t * TILE, TILE), :]).then_inc(g.x_loaded, 16)
                        sp.wait_ge(g.node_done, t + 1)
                        sp.nop(nofuse=True)
                    sp.wait_ge(g.nat_copied, 1)
                    sp.dma_start(st_dram[l].rearrange("c (t m) -> (c t) m", m=TILE), nat_t[:]).then_inc(g.st_stored, 16)
                    sp.wait_ge(g.st_stored, 16)
                    sp.dma_start(t_wide, st_dram[l][1, :].partition_broadcast(128)).then_inc(g.t_loaded, 16)
                    with sp.Fori(0, TILES) as t:
                        sp.dma_start(adj_rows, adj[ds(t * TILE, TILE), :]).then_inc(g.rows_loaded, 16)
                        sp.dma_start(x_old[:, 0, :], x_src[l][ds(t * TILE, TILE), :]).then_inc(g.rows_loaded, 16)
                        sp.wait_ge(g.x_done, t + 1)
                        sp.nop(nofuse=True)
                        sp.dma_start(x_dst[l][ds(t * TILE, TILE), :], x_new[:, 0, :]).then_inc(g.x_stored, 16)
                        sp.wait_ge(g.x_stored, 16 * t + 16)
                        sp.nop(nofuse=True)

        @general_block.gpsimd
        def _(pool):
            with pool.If(pool.value_load(use_general[0:1, 0:1]) > 0):
                for l in range(LAYERS):
                    with pool.Fori(0, TILES) as t:
                        pool.wait_ge(G[l].x_normal, t + 1)
                        pool.nop(nofuse=True)
                        pool.tensor_tensor(rstd[:, 0, :], var_eps[:, 0, :], minus_half[:], ALU.pow).then_inc(G[l].scaled, 1)

        @general_block.tensor
        def _(pe):
            with pe.If(pe.value_load(use_general[0:1, 0:1]) > 0):
                for l in range(LAYERS):
                    g = G[l]
                    with pe.Fori(0, TILES) as t:
                        pe.wait_ge(g.x_normal, t + 1)
                        pe.nop(nofuse=True)
                        pe.transpose(ps_t[0][:, 0:DIM], centred[:, 0, :], ident[:]).then_inc(g.turned, 1)
                        pe.wait_ge(g.copied, t + 1)
                        pe.nop(nofuse=True)
                        pe.matmul(ps_h[:, 0:EXT], centred_t[:, 0, :], w_ext[l][:], start=True, stop=True) \
                          .then_inc(g.projected, 1)
                        pe.wait_ge(g.node_done, t + 1)
                        pe.nop(nofuse=True)
                    pe.transpose(ps_t[0][:, 0:128], nat[:], ident[:]).then_inc(g.nat_turned, 1)
                    pe.wait_ge(g.nat_copied, 1)
                    with pe.Fori(0, TILES) as t:
                        pe.wait_ge(g.exp_done, t + 1)
                        pe.nop(nofuse=True)

                        for c in range(TILES):
                            pe.transpose(ps_t[0][:, 0:TILE], score[:, c * TILE:(c + 1) * TILE], ident[:]).then_inc(g.p_turned, 1)
                            pe.wait_ge(g.p_copied, TILES * t + c + 1)
                            pe.nop(nofuse=True)
                            pe.matmul(acc[0][0][:, 0:DIM], centred_t[:, 0, :], h_all[:, c, :],
                                      start=(c == 0), stop=(c == TILES - 1), skip_group_check=True).then_inc(g.p_used, 1)
                            pe.wait_ge(g.p_used, TILES * t + c + 1)
                            pe.nop(nofuse=True)
                        pe.wait_ge(g.x_done, t + 1)
                        pe.nop(nofuse=True)

        @general_block.scalar
        def _(act):
            with act.If(act.value_load(use_general[0:1, 0:1]) > 0):
                for l in range(LAYERS):
                    g = G[l]
                    with act.Fori(0, TILES) as t:
                        act.wait_ge(g.turned, t + 1)
                        act.nop(nofuse=True)
                        nc.scalar.copy(centred_t[:, 0, :], ps_t[0][:, 0:DIM]).then_inc(g.copied, 1)
                        act.wait_ge(g.node_done, t + 1)
                        act.nop(nofuse=True)
                    with act.Fori(0, TILES) as t:
                        act.wait_ge(g.shifted, t + 1)
                        act.nop(nofuse=True)
                        nc.scalar.activation(score, score, ACT.Exp).then_inc(g.exp_done, 1)
                        with act.Fori(0, TILES) as c:
                            act.wait_ge(g.p_turned, TILES * t + c + 1)
                            act.nop(nofuse=True)
                            nc.scalar.copy(centred_t[:, 0, :], ps_t[0][:, 0:TILE]).then_inc(g.p_copied, 1)
                            act.wait_ge(g.p_used, TILES * t + c + 1)
                            act.nop(nofuse=True)

        @general_block.vector
        def _(dve):
            node_steps, row_steps = 5, 7
            with dve.If(dve.value_load(use_general[0:1, 0:1]) > 0):
                for l in range(LAYERS):
                    g = G[l]
                    with dve.Fori(0, TILES) as t:
                        step = in_order(dve, g.node_steps, node_steps * t, node_steps)
                        dve.wait_ge(g.x_loaded, 16 * t + 16)
                        dve.nop(nofuse=True)
                        step(nc.vector.bn_stats(stats[:, 0, :], x_old[:, 0, :]))
                        step(nc.vector.bn_aggr(mean_var[:, 0, :], stats[:, 0, :]))
                        step(nc.vector.tensor_scalar(centred[:, 0, :], x_old[:, 0, :], mean_var[:, 0, 0:1], 0.0,
                                                     ALU.subtract, ALU.max))
                        nc.vector.tensor_scalar(var_eps[:, 0, :], mean_var[:, 0, 1:2], EPS, None, ALU.add).then_inc(g.x_normal, 1)
                        dve.wait_ge(g.scaled, t + 1)
                        dve.wait_ge(g.projected, t + 1)
                        dve.nop(nofuse=True)
                        step(nc.vector.scalar_tensor_tensor(out=ext[:, 0, :], in0=ps_h[:, 0:EXT], scalar=rstd[:, 0, :],
                                                            in1=bias[l][:], op0=ALU.mult, op1=ALU.add))
                        step(nc.vector.tensor_copy(nat[:].rearrange("p (c t) -> p c t", c=2)[:, :, ds(t, 1)],
                                                   ext[:, 0, NEG_S:POS_T + 1].rearrange("p (c o) -> p c o", o=1)))
                        nc.vector.tensor_copy(h_all[:, ds(t, 1), :].rearrange("p o d -> p (o d)"), ext[:, 0, 0:DIM]) \
                            .then_inc(g.node_done, 1)
                        dve.wait_ge(g.node_done, t + 1)
                        dve.nop(nofuse=True)
                    dve.wait_ge(g.nat_turned, 1)
                    nc.vector.tensor_copy(nat_t[:], ps_t[0][:, 0:128]).then_inc(g.nat_copied, 1)
                    dve.wait_ge(g.t_loaded, 16)
                    with dve.Fori(0, TILES) as t:
                        step = in_order(dve, g.row_steps, row_steps * t, row_steps)
                        dve.wait_ge(g.rows_loaded, 32 * t + 32)
                        dve.nop(nofuse=True)
                        step(nc.vector.tensor_scalar(score, t_wide, scalar_of[:, ds(t, 1)], None, ALU.subtract))
                        step(nc.vector.scalar_tensor_tensor(out=score, in0=score, scalar=LEAK, in1=score,
                                                            op0=ALU.mult, op1=ALU.max))
                        step(nc.vector.tensor_scalar(limit, adj_rows, 0.0, 2 * NO_EDGE, ALU.is_gt, ALU.mult))
                        step(nc.vector.scalar_tensor_tensor(out=score, in0=limit, scalar=-NO_EDGE, in1=score,
                                                            op0=ALU.add, op1=ALU.min))
                        step(nc.vector.tensor_reduce(row_max, score, AX.X, ALU.max))
                        nc.vector.tensor_scalar(score, score, row_max, None, ALU.subtract).then_inc(g.shifted, 1)
                        dve.wait_ge(g.exp_done, t + 1)
                        dve.nop(nofuse=True)
                        step(nc.vector.tensor_reduce(row_sum, score, AX.X, ALU.add))
                        step(nc.vector.reciprocal(row_scale, row_sum))
                        dve.wait_ge(g.p_used, TILES * t + TILES)
                        dve.nop(nofuse=True)
                        nc.vector.scalar_tensor_tensor(out=x_new[:, 0, :], in0=acc[0][0][:, 0:DIM], scalar=row_scale,
                                                       in1=x_old[:, 0, :], op0=ALU.mult, op1=ALU.add).then_inc(g.x_done, 1)
                        dve.wait_ge(g.x_done, t + 1)
                        dve.nop(nofuse=True)


_INS = ['x', 'adj', 'L0_gnn_W', 'L0_gnn_b_W', 'L0_gnn_a_vec', 'L0_gnn_b_a', 'L1_gnn_W_w', 'L1_gnn_W_b', 'L1_gnn_a']


def kernel(**inputs):
    import numpy as _np
    import concourse.bacc as _bacc
    from concourse import mybir as _mybir
    from concourse.bass_utils import run_bass_kernel_spmd as _run

    nc = _bacc.Bacc("TRN2", target_bir_lowering=False, num_devices=1)
    arrays, args = {}, []
    for name in _INS:
        a = _np.ascontiguousarray(inputs[name])
        arrays[f"in_{name}_dram"] = a
        args.append(nc.dram_tensor(f"in_{name}_dram", a.shape, _mybir.dt.from_np(a.dtype), kind="ExternalInput").ap())
    args.append(nc.dram_tensor("out_0_dram", (NODES, DIM), _mybir.dt.float32, kind="ExternalOutput").ap())
    gat_kernel(nc, *args)
    r = _run(nc, [arrays], core_ids=[0])
    return r.results[0]["out_0_dram"]
```
